# Optimizing a Trainium2 kernel written in Bass

```python
import numpy as np
import jax
import jax.numpy as jnp

def _softmax(x, axis=-1):
    return jax.nn.softmax(x, axis=axis)

def _gelu(x):
    return jax.nn.gelu(x, approximate=True)

def _silu(x):
    return jax.nn.silu(x)

def _sigmoid(x):
    return jax.nn.sigmoid(x)

def _layernorm(x, axis=-1, eps=1e-05):
    m = jnp.mean(x, axis=axis, keepdims=True)
    v = jnp.var(x, axis=axis, keepdims=True)
    return (x - m) / jnp.sqrt(v + eps)

def _scatter_add(tgt, idx, src, axis=0):
    return tgt.at[idx].add(src)

def _segment_sum(src, seg, n):
    return jax.ops.segment_sum(src, seg, n)
kernel_name = 'mk_metaformer_d2_conv_nchw128_r4_ab1854'

def setup_inputs(seed: int=0):
    np.random.seed(seed)
    _w = jnp.asarray

    def _rec_inputs():
        import jax
        import jax.numpy as jnp
        _gk = jax.random.key(seed)
        x = -0.0003929 + 0.9999 * jax.random.normal(jax.random.fold_in(_gk, 1), (2, 32, 64, 64), jnp.float32)
        return x
    x = _rec_inputs()

    def _L0_conv_setup():
        import jax, jax.numpy as jnp
        import numpy as np
        from jax import lax
        BN_EPS = 0.001
        BN_S = float(1.0 / np.sqrt(1.0 + BN_EPS))
        DN = ('NCHW', 'OIHW', 'NCHW')

        def conv3(x, w, stride):
            return lax.conv_general_dilated(x, w, (stride, stride), [(1, 1), (1, 1)], dimension_numbers=DN)

        def conv1x1(x, w, stride):
            return lax.conv_general_dilated(x, w, (stride, stride), [(0, 0), (0, 0)], dimension_numbers=DN)

        def deconv2(x, w):
            n, c, h, wd = x.shape
            y = jnp.einsum('nchw,cokl->nohkwl', x, w)
            return y.reshape(n, w.shape[1], 2 * h, 2 * wd)

        def basic_block(x, w1, w2, stride=1, ds=None):
            out = jax.nn.relu(conv3(x, w1, stride) * BN_S)
            out = conv3(out, w2, 1) * BN_S
            identity = conv1x1(x, ds, stride) * BN_S if ds is not None else x
            return jax.nn.relu(out + identity)
        key = jax.random.key(seed)
        ks = jax.random.split(key, 18)
        D = 32
        w33 = lambda k: jax.random.normal(k, (D, D, 3, 3), jnp.float32) * 0.04
        w11 = lambda k: jax.random.normal(k, (D, D, 1, 1), jnp.float32) * 0.12
        wT = lambda k: jax.random.normal(k, (D, D, 2, 2), jnp.float32) * 0.06
        return {'x': jax.random.normal(ks[0], (2, D, 64, 64), jnp.float32), 'e0b0c1': w33(ks[1]), 'e0b0c2': w33(ks[2]), 'e0b1c1': w33(ks[3]), 'e0b1c2': w33(ks[4]), 'e1b0c1': w33(ks[5]), 'e1b0c2': w33(ks[6]), 'e1b0ds': w11(ks[7]), 'e1b1c1': w33(ks[8]), 'e1b1c2': w33(ks[9]), 'e2b0c1': w33(ks[10]), 'e2b0c2': w33(ks[11]), 'e2b0ds': w11(ks[12]), 'e2b1c1': w33(ks[13]), 'e2b1c2': w33(ks[14]), 'dec0w': wT(ks[15]), 'dec1w': wT(ks[16])}
    _L0_conv_all = _L0_conv_setup()
    _L0_conv_in = {k: v for k, v in _L0_conv_all.items() if k in ('e0b0c1', 'e0b0c2', 'e0b1c1', 'e0b1c2', 'e1b0c1', 'e1b0c2', 'e1b0ds', 'e1b1c1', 'e1b1c2', 'e2b0c1', 'e2b0c2', 'e2b0ds', 'e2b1c1', 'e2b1c2', 'dec0w', 'dec1w')}
    del _L0_conv_all

    def _L0_ffn_setup():
        import jax, jax.numpy as jnp
        import numpy as np
        B, S, D, E, H, O, K = (128, 512, 32, 16, 128, 32, 8)
        key = jax.random.key(seed)
        k0, k1, k2, k3 = jax.random.split(key, 4)
        x = jax.random.normal(k0, (B, S, D), dtype=jnp.float32)
        gate_w = jax.random.normal(k1, (E, D), dtype=jnp.float32) * (1.0 / np.sqrt(D))
        gate_b = jnp.zeros((E,), dtype=jnp.float32)
        weight1 = jax.random.uniform(k2, (E, D + 1, H), dtype=jnp.float32, minval=-1.0, maxval=1.0) * (1.0 / np.sqrt(D + 1))
        weight2 = jax.random.uniform(k3, (E, H + 1, O), dtype=jnp.float32, minval=-1.0, maxval=1.0) * (1.0 / np.sqrt(H + 1))
        return {'x': x, 'gate_w': gate_w, 'gate_b': gate_b, 'weight1': weight1, 'weight2': weight2}
    _L0_ffn_all = _L0_ffn_setup()
    _L0_ffn_in = {k: v for k, v in _L0_ffn_all.items() if k in ('gate_w', 'gate_b', 'weight1', 'weight2')}
    del _L0_ffn_all

    def _L1_conv_setup():
        import jax, jax.numpy as jnp
        import numpy as np
        G = 4
        K = 9
        EPS = 1e-05

        def _bilinear_gather(value, loc_y, loc_x):
            N, H, W, g, Cg = value.shape
            y0f = jnp.floor(loc_y)
            x0f = jnp.floor(loc_x)
            wy = loc_y - y0f
            wx = loc_x - x0f
            y0 = y0f.astype(jnp.int32)
            x0 = x0f.astype(jnp.int32)
            n_idx = jnp.arange(N).reshape(N, 1, 1, 1, 1)
            g_idx = jnp.arange(g).reshape(1, 1, 1, g, 1)

            def corner(yi, xi, w):
                valid = (yi >= 0) & (yi < H) & (xi >= 0) & (xi < W)
                yc = jnp.clip(yi, 0, H - 1)
                xc = jnp.clip(xi, 0, W - 1)
                v = value[n_idx, yc, xc, g_idx]
                return v * (w * valid)[..., None]
            return corner(y0, x0, (1 - wy) * (1 - wx)) + corner(y0, x0 + 1, (1 - wy) * wx) + corner(y0 + 1, x0, wy * (1 - wx)) + corner(y0 + 1, x0 + 1, wy * wx)

        def _dcnv4(t, H, W, Wv, bv, Wom, bom, Wo):
            N, L, C = t.shape
            Cg = C // G
            value = (t @ Wv + bv).reshape(N, H, W, G, Cg)
            om = (t @ Wom + bom).reshape(N, H, W, G, 3 * K)
            offset = om[..., :2 * K].reshape(N, H, W, G, K, 2)
            mask = om[..., 2 * K:]
            ky, kx = jnp.meshgrid(jnp.arange(-1, 2), jnp.arange(-1, 2), indexing='ij')
            ky = ky.reshape(-1).astype(t.dtype)
            kx = kx.reshape(-1).astype(t.dtype)
            ys = jnp.arange(H, dtype=t.dtype).reshape(1, H, 1, 1, 1)
            xs = jnp.arange(W, dtype=t.dtype).reshape(1, 1, W, 1, 1)
            loc_y = ys + ky + offset[..., 1]
            loc_x = xs + kx + offset[..., 0]
            sampled = _bilinear_gather(value, loc_y, loc_x)
            out = (sampled * mask[..., None]).sum(axis=4)
            return out.reshape(N, L, C) @ Wo

        def _bn(x, gamma, beta):
            mean = x.mean(axis=(0, 2, 3), keepdims=True)
            var = ((x - mean) ** 2).mean(axis=(0, 2, 3), keepdims=True)
            return (x - mean) * jax.lax.rsqrt(var + EPS) * gamma.reshape(1, -1, 1, 1) + beta.reshape(1, -1, 1, 1)
        key = jax.random.key(seed)
        ks = jax.random.split(key, 6)
        N, C, H, W = (4, 32, 16, 16)
        s = 1.0 / np.sqrt(C)
        x = jax.random.normal(ks[0], (N, C, H, W), jnp.float32)
        Wv = jax.random.normal(ks[1], (C, C), jnp.float32) * s
        bv = jnp.zeros((C,), jnp.float32)
        Wom = jax.random.normal(ks[2], (C, G * 3 * K), jnp.float32) * 0.01
        bom = jnp.zeros((G * 3 * K,), jnp.float32)
        Wo = jax.random.normal(ks[3], (C, C), jnp.float32) * s
        gamma = jnp.ones((C,), jnp.float32)
        beta = jnp.zeros((C,), jnp.float32)
        Wc = jax.random.normal(ks[4], (C, C), jnp.float32) * s
        return {'x': x, 'Wv': Wv, 'bv': bv, 'Wom': Wom, 'bom': bom, 'Wo': Wo, 'gamma': gamma, 'beta': beta, 'Wc': Wc}
    _L1_conv_all = _L1_conv_setup()
    _L1_conv_in = {k: v for k, v in _L1_conv_all.items() if k in ('Wv', 'bv', 'Wom', 'bom', 'Wo', 'gamma', 'beta', 'Wc')}
    del _L1_conv_all

    def _L1_ffn_setup():
        import jax, jax.numpy as jnp
        import numpy as np
        B, S, D, E, H, O, K = (128, 512, 32, 16, 128, 32, 8)
        key = jax.random.key(seed)
        k0, k1, k2, k3 = jax.random.split(key, 4)
        x = jax.random.normal(k0, (B, S, D), dtype=jnp.float32)
        gate_w = jax.random.normal(k1, (E, D), dtype=jnp.float32) * (1.0 / np.sqrt(D))
        gate_b = jnp.zeros((E,), dtype=jnp.float32)
        weight1 = jax.random.uniform(k2, (E, D + 1, H), dtype=jnp.float32, minval=-1.0, maxval=1.0) * (1.0 / np.sqrt(D + 1))
        weight2 = jax.random.uniform(k3, (E, H + 1, O), dtype=jnp.float32, minval=-1.0, maxval=1.0) * (1.0 / np.sqrt(H + 1))
        return {'x': x, 'gate_w': gate_w, 'gate_b': gate_b, 'weight1': weight1, 'weight2': weight2}
    _L1_ffn_all = _L1_ffn_setup()
    _L1_ffn_in = {k: v for k, v in _L1_ffn_all.items() if k in ('gate_w', 'gate_b', 'weight1', 'weight2')}
    del _L1_ffn_all
    return {'x': x, 'L0_conv_e0b0c1': _L0_conv_in['e0b0c1'], 'L0_conv_e0b0c2': _L0_conv_in['e0b0c2'], 'L0_conv_e0b1c1': _L0_conv_in['e0b1c1'], 'L0_conv_e0b1c2': _L0_conv_in['e0b1c2'], 'L0_conv_e1b0c1': _L0_conv_in['e1b0c1'], 'L0_conv_e1b0c2': _L0_conv_in['e1b0c2'], 'L0_conv_e1b0ds': _L0_conv_in['e1b0ds'], 'L0_conv_e1b1c1': _L0_conv_in['e1b1c1'], 'L0_conv_e1b1c2': _L0_conv_in['e1b1c2'], 'L0_conv_e2b0c1': _L0_conv_in['e2b0c1'], 'L0_conv_e2b0c2': _L0_conv_in['e2b0c2'], 'L0_conv_e2b0ds': _L0_conv_in['e2b0ds'], 'L0_conv_e2b1c1': _L0_conv_in['e2b1c1'], 'L0_conv_e2b1c2': _L0_conv_in['e2b1c2'], 'L0_conv_dec0w': _L0_conv_in['dec0w'], 'L0_conv_dec1w': _L0_conv_in['dec1w'], 'L0_ffn_gate_w': _L0_ffn_in['gate_w'], 'L0_ffn_gate_b': _L0_ffn_in['gate_b'], 'L0_ffn_weight1': _L0_ffn_in['weight1'], 'L0_ffn_weight2': _L0_ffn_in['weight2'], 'L1_conv_Wv': _L1_conv_in['Wv'], 'L1_conv_bv': _L1_conv_in['bv'], 'L1_conv_Wom': _L1_conv_in['Wom'], 'L1_conv_bom': _L1_conv_in['bom'], 'L1_conv_Wo': _L1_conv_in['Wo'], 'L1_conv_gamma': _L1_conv_in['gamma'], 'L1_conv_beta': _L1_conv_in['beta'], 'L1_conv_Wc': _L1_conv_in['Wc'], 'L1_ffn_gate_w': _L1_ffn_in['gate_w'], 'L1_ffn_gate_b': _L1_ffn_in['gate_b'], 'L1_ffn_weight1': _L1_ffn_in['weight1'], 'L1_ffn_weight2': _L1_ffn_in['weight2']}

def reference(x, L0_conv_e0b0c1, L0_conv_e0b0c2, L0_conv_e0b1c1, L0_conv_e0b1c2, L0_conv_e1b0c1, L0_conv_e1b0c2, L0_conv_e1b0ds, L0_conv_e1b1c1, L0_conv_e1b1c2, L0_conv_e2b0c1, L0_conv_e2b0c2, L0_conv_e2b0ds, L0_conv_e2b1c1, L0_conv_e2b1c2, L0_conv_dec0w, L0_conv_dec1w, L0_ffn_gate_w, L0_ffn_gate_b, L0_ffn_weight1, L0_ffn_weight2, L1_conv_Wv, L1_conv_bv, L1_conv_Wom, L1_conv_bom, L1_conv_Wo, L1_conv_gamma, L1_conv_beta, L1_conv_Wc, L1_ffn_gate_w, L1_ffn_gate_b, L1_ffn_weight1, L1_ffn_weight2):
    import jax
    import jax.numpy as jnp

    def _L0_conv_ref(x, e0b0c1, e0b0c2, e0b1c1, e0b1c2, e1b0c1, e1b0c2, e1b0ds, e1b1c1, e1b1c2, e2b0c1, e2b0c2, e2b0ds, e2b1c1, e2b1c2, dec0w, dec1w):
        import jax, jax.numpy as jnp
        import numpy as np
        from jax import lax
        BN_EPS = 0.001
        BN_S = float(1.0 / np.sqrt(1.0 + BN_EPS))
        DN = ('NCHW', 'OIHW', 'NCHW')

        def conv3(x, w, stride):
            return lax.conv_general_dilated(x, w, (stride, stride), [(1, 1), (1, 1)], dimension_numbers=DN)

        def conv1x1(x, w, stride):
            return lax.conv_general_dilated(x, w, (stride, stride), [(0, 0), (0, 0)], dimension_numbers=DN)

        def deconv2(x, w):
            n, c, h, wd = x.shape
            y = jnp.einsum('nchw,cokl->nohkwl', x, w)
            return y.reshape(n, w.shape[1], 2 * h, 2 * wd)

        def basic_block(x, w1, w2, stride=1, ds=None):
            out = jax.nn.relu(conv3(x, w1, stride) * BN_S)
            out = conv3(out, w2, 1) * BN_S
            identity = conv1x1(x, ds, stride) * BN_S if ds is not None else x
            return jax.nn.relu(out + identity)
        x = basic_block(x, e0b0c1, e0b0c2)
        x = basic_block(x, e0b1c1, e0b1c2)
        f0 = x
        x = basic_block(x, e1b0c1, e1b0c2, stride=2, ds=e1b0ds)
        x = basic_block(x, e1b1c1, e1b1c2)
        f1 = x
        x = basic_block(x, e2b0c1, e2b0c2, stride=2, ds=e2b0ds)
        x = basic_block(x, e2b1c1, e2b1c2)
        x = (jax.nn.relu(deconv2(x, dec0w) * BN_S) + f1) * BN_S
        x = (jax.nn.relu(deconv2(x, dec1w) * BN_S) + f0) * BN_S
        return x

    def _L0_ffn_ref(x, gate_w, gate_b, weight1, weight2):
        import jax, jax.numpy as jnp
        import numpy as np
        B, S, D, E, H, O, K = (128, 512, 32, 16, 128, 32, 8)
        Bn, Sn, Dn = x.shape
        logits = jnp.einsum('bsd,ed->bse', x, gate_w) + gate_b
        probs = jax.nn.softmax(logits, axis=1)
        vals, idx = jax.lax.top_k(probs.transpose(0, 2, 1), K)
        topv = vals.transpose(0, 2, 1)
        topi = idx.transpose(0, 2, 1)
        flat_idx = topi.reshape(Bn, K * E)
        gathered = jnp.take_along_axis(x, flat_idx[:, :, None], axis=1)
        gathered = gathered.reshape(Bn, K, E, Dn)
        pooled = jnp.einsum('bked,bke->bed', gathered, topv)
        ones = jnp.ones((E, Bn, 1), dtype=x.dtype)
        h = jnp.concatenate([pooled.transpose(1, 0, 2), ones], axis=-1)
        h = jax.nn.gelu(jnp.einsum('ebd,edh->ebh', h, weight1), approximate=False)
        h = jnp.concatenate([h, ones], axis=-1)
        out = jnp.einsum('ebh,eho->ebo', h, weight2)
        out = out.transpose(1, 0, 2)
        weighted = jnp.einsum('beo,bke->bkeo', out, topv).reshape(Bn, K * E, O)
        outputs = jnp.zeros((Bn, Sn, O), dtype=x.dtype)
        outputs = outputs.at[jnp.arange(Bn)[:, None], flat_idx].add(weighted)
        return outputs

    def _L1_conv_ref(x, Wv, bv, Wom, bom, Wo, gamma, beta, Wc):
        import jax, jax.numpy as jnp
        import numpy as np
        G = 4
        K = 9
        EPS = 1e-05

        def _bilinear_gather(value, loc_y, loc_x):
            N, H, W, g, Cg = value.shape
            y0f = jnp.floor(loc_y)
            x0f = jnp.floor(loc_x)
            wy = loc_y - y0f
            wx = loc_x - x0f
            y0 = y0f.astype(jnp.int32)
            x0 = x0f.astype(jnp.int32)
            n_idx = jnp.arange(N).reshape(N, 1, 1, 1, 1)
            g_idx = jnp.arange(g).reshape(1, 1, 1, g, 1)

            def corner(yi, xi, w):
                valid = (yi >= 0) & (yi < H) & (xi >= 0) & (xi < W)
                yc = jnp.clip(yi, 0, H - 1)
                xc = jnp.clip(xi, 0, W - 1)
                v = value[n_idx, yc, xc, g_idx]
                return v * (w * valid)[..., None]
            return corner(y0, x0, (1 - wy) * (1 - wx)) + corner(y0, x0 + 1, (1 - wy) * wx) + corner(y0 + 1, x0, wy * (1 - wx)) + corner(y0 + 1, x0 + 1, wy * wx)

        def _dcnv4(t, H, W, Wv, bv, Wom, bom, Wo):
            N, L, C = t.shape
            Cg = C // G
            value = (t @ Wv + bv).reshape(N, H, W, G, Cg)
            om = (t @ Wom + bom).reshape(N, H, W, G, 3 * K)
            offset = om[..., :2 * K].reshape(N, H, W, G, K, 2)
            mask = om[..., 2 * K:]
            ky, kx = jnp.meshgrid(jnp.arange(-1, 2), jnp.arange(-1, 2), indexing='ij')
            ky = ky.reshape(-1).astype(t.dtype)
            kx = kx.reshape(-1).astype(t.dtype)
            ys = jnp.arange(H, dtype=t.dtype).reshape(1, H, 1, 1, 1)
            xs = jnp.arange(W, dtype=t.dtype).reshape(1, 1, W, 1, 1)
            loc_y = ys + ky + offset[..., 1]
            loc_x = xs + kx + offset[..., 0]
            sampled = _bilinear_gather(value, loc_y, loc_x)
            out = (sampled * mask[..., None]).sum(axis=4)
            return out.reshape(N, L, C) @ Wo

        def _bn(x, gamma, beta):
            mean = x.mean(axis=(0, 2, 3), keepdims=True)
            var = ((x - mean) ** 2).mean(axis=(0, 2, 3), keepdims=True)
            return (x - mean) * jax.lax.rsqrt(var + EPS) * gamma.reshape(1, -1, 1, 1) + beta.reshape(1, -1, 1, 1)
        N, C, H, W = x.shape
        shortcut = x
        t = x.transpose(0, 2, 3, 1).reshape(N, H * W, C)
        t = _dcnv4(t, H, W, Wv, bv, Wom, bom, Wo)
        y = t.reshape(N, H, W, C).transpose(0, 3, 1, 2)
        y = jax.nn.relu(_bn(y, gamma, beta))
        t = y.transpose(0, 2, 3, 1).reshape(N, H * W, C)
        t = _dcnv4(t, H, W, Wv, bv, Wom, bom, Wo)
        y = t.reshape(N, H, W, C).transpose(0, 3, 1, 2)
        y = _bn(y, gamma, beta)
        y = y + shortcut
        return jnp.einsum('nchw,oc->nohw', y, Wc)

    def _L1_ffn_ref(x, gate_w, gate_b, weight1, weight2):
        import jax, jax.numpy as jnp
        import numpy as np
        B, S, D, E, H, O, K = (128, 512, 32, 16, 128, 32, 8)
        Bn, Sn, Dn = x.shape
        logits = jnp.einsum('bsd,ed->bse', x, gate_w) + gate_b
        probs = jax.nn.softmax(logits, axis=1)
        vals, idx = jax.lax.top_k(probs.transpose(0, 2, 1), K)
        topv = vals.transpose(0, 2, 1)
        topi = idx.transpose(0, 2, 1)
        flat_idx = topi.reshape(Bn, K * E)
        gathered = jnp.take_along_axis(x, flat_idx[:, :, None], axis=1)
        gathered = gathered.reshape(Bn, K, E, Dn)
        pooled = jnp.einsum('bked,bke->bed', gathered, topv)
        ones = jnp.ones((E, Bn, 1), dtype=x.dtype)
        h = jnp.concatenate([pooled.transpose(1, 0, 2), ones], axis=-1)
        h = jax.nn.gelu(jnp.einsum('ebd,edh->ebh', h, weight1), approximate=False)
        h = jnp.concatenate([h, ones], axis=-1)
        out = jnp.einsum('ebh,eho->ebo', h, weight2)
        out = out.transpose(1, 0, 2)
        weighted = jnp.einsum('beo,bke->bkeo', out, topv).reshape(Bn, K * E, O)
        outputs = jnp.zeros((Bn, Sn, O), dtype=x.dtype)
        outputs = outputs.at[jnp.arange(Bn)[:, None], flat_idx].add(weighted)
        return outputs

    def _gn(v, G=32, eps=1e-05):
        B_, C_, H_, W_ = v.shape
        g = v.reshape(B_, G, C_ // G, H_, W_)
        m = jnp.mean(g, axis=(2, 3, 4), keepdims=True)
        s = jnp.var(g, axis=(2, 3, 4), keepdims=True)
        return ((g - m) / jnp.sqrt(s + eps)).reshape(v.shape)

    def _ln_c(v, eps=1e-06):
        m = jnp.mean(v, axis=1, keepdims=True)
        s = jnp.var(v, axis=1, keepdims=True)
        return (v - m) / jnp.sqrt(s + eps)

    def _ln_t(v, eps=1e-05):
        m = jnp.mean(v, axis=-1, keepdims=True)
        s = jnp.var(v, axis=-1, keepdims=True)
        return (v - m) / jnp.sqrt(s + eps)

    def _to_tokens(v):
        B_, C_, H_, W_ = v.shape
        return v.reshape(B_, C_, H_ * W_).transpose(0, 2, 1)

    def _from_tokens(t, like):
        B_, C_, H_, W_ = like.shape
        return t.transpose(0, 2, 1).reshape(B_, C_, H_, W_)
    x = x + _L0_conv_ref(_ln_c(x), L0_conv_e0b0c1, L0_conv_e0b0c2, L0_conv_e0b1c1, L0_conv_e0b1c2, L0_conv_e1b0c1, L0_conv_e1b0c2, L0_conv_e1b0ds, L0_conv_e1b1c1, L0_conv_e1b1c2, L0_conv_e2b0c1, L0_conv_e2b0c2, L0_conv_e2b0ds, L0_conv_e2b1c1, L0_conv_e2b1c2, L0_conv_dec0w, L0_conv_dec1w)
    t = _to_tokens(x)
    t = t + _L0_ffn_ref(_ln_t(t), L0_ffn_gate_w, L0_ffn_gate_b, L0_ffn_weight1, L0_ffn_weight2)
    x = _from_tokens(t, x)
    x = x + _L1_conv_ref(_ln_c(x), L1_conv_Wv, L1_conv_bv, L1_conv_Wom, L1_conv_bom, L1_conv_Wo, L1_conv_gamma, L1_conv_beta, L1_conv_Wc)
    t = _to_tokens(x)
    t = t + _L1_ffn_ref(_ln_t(t), L1_ffn_gate_w, L1_ffn_gate_b, L1_ffn_weight1, L1_ffn_weight2)
    x = _from_tokens(t, x)
    return x

_drawn_inputs = setup_inputs


def setup_inputs(seed=0):
    import zlib

    import numpy as np

    out = dict(_drawn_inputs(seed))
    spreads = {'L0_ffn_gate_b': (0.0, 2.0),
     'L1_conv_bv': (0.0, 2.0),
     'L1_conv_bom': (0.0, 0.8),
     'L1_conv_gamma': (1.0, 0.6),
     'L1_conv_beta': (0.0, 0.8),
     'L1_ffn_gate_b': (0.0, 0.1)}
    factors = {'L0_conv_e1b0c1': 2.849,
     'L0_conv_e1b1c1': 4.153,
     'L0_conv_e1b1c2': 3.432,
     'L0_conv_e2b0c1': 8.0,
     'L0_conv_e2b0c2': 8.0,
     'L0_conv_e2b0ds': 8.0,
     'L0_conv_e2b1c1': 8.0,
     'L0_conv_e2b1c2': 8.0,
     'L0_conv_dec0w': 6.614,
     'L0_ffn_gate_w': 64.0,
     'L0_ffn_weight1': 64.0,
     'L0_ffn_weight2': 64.0,
     'L1_ffn_gate_w': 64.0,
     'L1_ffn_weight1': 64.0,
     'L1_ffn_weight2': 64.0,
     'L1_conv_Wv': 8.0,
     'L1_conv_Wom': 8.0,
     'L1_conv_Wo': 8.0,
     'L1_conv_Wc': 8.0}
    for name, (base, spread) in spreads.items():
        noise = np.random.default_rng([zlib.crc32(name.encode()), seed]).standard_normal(out[name].shape)
        drawn = base * np.exp(spread * noise) if base else spread * noise
        out[name] = jnp.asarray(drawn.astype(out[name].dtype))
    for name, factor in factors.items():
        out[name] = (out[name] * factor).astype(out[name].dtype)
    return out
```

```python
from contextlib import ExitStack

import numpy as np

import concourse.bass as bass
from concourse import mybir

F32 = mybir.dt.float32
I32 = mybir.dt.int32
ALU = mybir.AluOpType
ACT = mybir.ActivationFunctionType
AX_X = mybir.AxisListType.X

NI, C, HW = 2, 32, 64
R = 4
NY = HW // R
COLS = NI * NY * HW
BANK = 512
NQ = COLS // BANK
EXP, TOPK, HID = 16, 8, 128
TOK = 1024
LOW = -3.0e38
G, K, CG = 4, 9, 8
TAPS = K * R * HW

XC, NXC, X0 = 10, 13, -65
NYP, YS0 = 66, -66
PROWS = 2 * NYP + HW
PCOLS = XC * NXC + HW
WB = HW + XC - 1
PLANE = PROWS * CG * PCOLS
STEPS = 2 * XC
FOLD = 3
ZERO = NI * G * PLANE // (128 * 4)

BN_S = float(1.0 / np.sqrt(1.0 + 0.001))

S1 = ["e0b0c1", "e0b0c2", "e0b1c1", "e0b1c2", "e1b0c2", "e1b1c1", "e1b1c2", "e2b0c2", "e2b1c1", "e2b1c2"]
S2 = ["e1b0c1", "e2b0c1"]
DS = ["e1b0ds", "e2b0ds"]
DEC = ["dec0w", "dec1w"]
RAW3 = (len(S1) + len(S2)) * 288
RAWN = RAW3 + 2 * 32 + 2 * 128


def columns(*sizes):
    at, out = 0, {}
    for name, n in sizes:
        out[name] = (at, at + n)
        at += n
    return out, at


CONST, NCONST = columns(
    ("ident", 128), ("chan_mean", 128), ("row_mean", 128), ("same_expert", 128), ("to_expert", 32),
    ("from_expert", 128), ("quarter", 4), ("parity", 2), ("rowsel", 4), ("colsel", 4), ("half", 4),
    ("eps6", 1), ("eps5", 1), ("tapoff", 1), ("ytab", 2 * NYP), ("xtab", XC * NXC),
    ("ylow", NYP), ("yhigh", NYP), ("xlow", NXC), ("xhigh", NXC))


def constants():
    t = np.zeros((128, NCONST), np.float32)

    def put(name, a):
        lo, hi = CONST[name]
        t[:a.shape[0], lo:hi] = a

    p = np.arange(128)
    put("ident", np.eye(128))
    put("chan_mean", (p[:, None] // 32 == p[None] // 32) / 32.0)
    put("row_mean", (p[:, None] % 32 == p[None] % 32) / 4.0)
    n, q, e = p // 64, p // 16 % 4, p % 16
    same = (n[:, None] == n[None]) & (e[:, None] == e[None])
    put("same_expert", same)
    m = np.arange(32)
    put("to_expert", (n[:, None] == m[None] // 16) & (e[:, None] == m[None] % 16))
    put("from_expert", (m[:, None] // 16 == n[None]) & (m[:, None] % 16 == e[None]))
    put("quarter", q[:, None] == np.arange(4)[None])
    put("parity", q[:, None] % 2 == np.arange(2)[None])
    put("rowsel", p[:, None] // 32 == np.arange(4)[None])
    put("colsel", p[:, None] // 8 % 4 == np.arange(4)[None])
    put("half", np.tile(np.eye(2).reshape(1, 4), (128, 1)))
    put("eps6", np.full((128, 1), 1e-6))
    put("eps5", np.full((128, 1), 1e-5))
    j = np.arange(108) % 27
    k = j % 9
    put("tapoff", np.where(j < 9, k % 3 - 1, np.where(j < 18, k // 3 - 1, 0))[:, None])
    ys = YS0 + np.arange(2 * NYP)
    xs = X0 + np.arange(XC * NXC)
    put("ytab", np.tile(-ys, (128, 1)))
    put("xtab", np.tile(-xs, (128, 1)))
    put("ylow", np.tile(-(ys[::2] + 2), (128, 1)))
    put("yhigh", np.tile(ys[::2] - 1, (128, 1)))
    put("xlow", np.tile(-(xs[::XC] + XC), (128, 1)))
    put("xhigh", np.tile(xs[::XC] - 1, (128, 1)))
    return t


def metaformer_kernel(nc, x, convw, gate_w, gate_b, w1, w2, w2b, wv, bv, wom, bom, wo, gamma, beta,
                      wct, consts, out, taps=None):
    with ExitStack() as ctx:
        def sb(name, shape, dt=F32):
            return ctx.enter_context(nc.sbuf_tensor(name, shape, dt))

        def sem(name):
            return ctx.enter_context(nc.semaphore(name))

        planes = nc.dram_tensor("planes", [NI * G * PLANE], F32, kind="Internal").ap()
        om_dram = nc.dram_tensor("om_dram", [108, NI, NY, R * HW], F32, kind="Internal").ap()
        smp_dram = nc.dram_tensor("smp_dram", [NI * G * NY, R * CG * HW], F32, kind="Internal").ap()
        short_dram = nc.dram_tensor("short_dram", [128, COLS], F32, kind="Internal").ap()

        X = sb("X", [128, COLS])
        cst = sb("cst", [128, NCONST])
        Wv_bd = sb("Wv_bd", [128, 128])
        Wo_bd = sb("Wo_bd", [128, 128])
        Wc_bd = sb("Wc_bd", [128, 128])
        Wom_r = sb("Wom_r", [128, 108])
        raw1 = sb("raw1", [128, 3, 32])
        vecs = sb("vecs", [128, 4])
        stats = sb("stats", [128, 4, 6])
        small = sb("small", [128, 16])
        ranges = sb("ranges", [1, 4], I32)
        arena = sb("arena", [128, 47936])

        def area(at, n):
            return arena[:, at:at + n]

        def const(name, parts=128):
            lo, hi = CONST[name]
            return cst[0:parts, lo:hi]

        ident = const("ident")
        raw = area(0, RAWN)
        Tw = area(3776, 3840)
        Sw = area(7616, 1536)
        Ew = area(9152, 512)
        Dw = area(30736, 1024)
        A = [area(10176 + i * 2376, 2376).rearrange("p (n y x) -> p n y x", n=NI, y=NY + 2) for i in range(3)]
        B = [area(26000 + i * 680, 680).rearrange("p (n y x) -> p n y x", n=NI, y=10) for i in range(3)]
        D = [area(28040 + i * 216, 216).rearrange("p (n y x) -> p n y x", n=NI, y=6) for i in range(3)]
        up = area(28688, 2048)
        XCt = area(19200, COLS)
        SQ = area(21248, COLS)
        U = area(23296, COLS)
        W1s = area(31760, 2048)[0:33, :].rearrange("p (e h) -> p e h", e=EXP)
        W2s = area(33808, 512).rearrange("p (e o) -> p e o", e=EXP)
        W2b = area(34320, 16)[0:32, :]
        gb = area(34336, 1)
        graw = area(34338, 16)
        Gw = area(34354, 256).rearrange("p (r h j) -> p r h j", r=R, h=2)
        Gh = area(34610, 64).rearrange("p (h j) -> p h j", h=2)
        LG = area(34680, 1032)
        LGr = area(35712, 1032)
        Ee = area(36744, 1024)
        E2 = area(37768, 1024)
        Pm = area(38792, 1024)
        XTs = area(39816, 2048).rearrange("p (j m) -> p j m", j=16)
        PTs = area(41864, 1024).rearrange("p (j m) -> p j m", j=8)
        FX = area(42888, 470)
        OMs = area(6912, 8192)[0:108, :].rearrange("p (n y r x) -> p n y r x", n=NI, y=NY, r=R)
        VAL = area(15104, COLS)
        T2 = area(17152, COLS)
        SMP = area(25344, COLS)
        SHT = area(27392, COLS)
        Zt = area(29440, COLS)
        dxy = area(0, 3 * TAPS)
        dx, dy, mk = (area(i * TAPS, TAPS) for i in range(3))
        hx = area(6912, XC * TAPS).rearrange("p (j t) -> p j t", j=XC)
        ay = area(29952, 2 * TAPS).rearrange("p (h t) -> p h t", h=2)
        Pt = area(34560, 2 * TAPS).rearrange("p (h t) -> p h t", h=2)
        Mt = area(39168, 2 * 2048).rearrange("p (h t) -> p h t", h=2)
        Vt = area(43264, 2 * 32 * WB).rearrange("p (h s w) -> p h s w", h=2, w=WB)
        zeros = area(36744, ZERO)
        zero_bank = area(43264, BANK)

        psA = ctx.enter_context(nc.psum_tensor("psA", [128, COLS], F32))
        psW = ctx.enter_context(nc.psum_tensor("psW", [128, 2, BANK], F32))
        T0 = ctx.enter_context(nc.psum_tensor("T0", [128, BANK], F32))
        T1 = ctx.enter_context(nc.psum_tensor("T1", [128, BANK], F32))

        x_in, cst_in, raw_in, small_in = sem("x_in"), sem("cst_in"), sem("raw_in"), sem("small_in")
        ffn_in = sem("ffn_in")
        zeroed, planes_zero = sem("zeroed"), sem("planes_zero")
        borders = sem("borders")
        w_zero, w_ready, t_ready = sem("w_zero"), sem("w_ready"), sem("t_ready")
        bd_ready = sem("bd_ready")
        ln_mean, ln_cent, ln_sq, ln_var = sem("ln_mean"), sem("ln_cent"), sem("ln_sq"), sem("ln_var")
        ln_std, ln_rstd, ln_out = sem("ln_std"), sem("ln_rstd"), sem("ln_out")
        conv_sum, evac_act, evac_dve, conv_res = sem("conv_sum"), sem("evac_act"), sem("evac_dve"), sem("conv_res")
        up_sum, up_relu, up_mix = sem("up_sum"), sem("up_relu"), sem("up_mix")
        x_upd = sem("x_upd")
        f_gw, f_xt, f_xts, f_lg, f_lgs = sem("f_gw"), sem("f_xt"), sem("f_xts"), sem("f_lg"), sem("f_lgs")
        f_top, f_ex, f_cand, f_ct, f_pack = sem("f_top"), sem("f_ex"), sem("f_cand"), sem("f_ct"), sem("f_pack")
        f_back, f_msk, f_max, f_rest = sem("f_back"), sem("f_msk"), sem("f_max"), sem("f_rest")
        f_exp, f_exp2, f_den, f_rden, f_dif, f_p = (sem("f_exp"), sem("f_exp2"), sem("f_den"), sem("f_rden"),
                                                    sem("f_dif"), sem("f_p"))
        f_pt, f_pts, f_pool, f_pooled = sem("f_pt"), sem("f_pts"), sem("f_pool"), sem("f_pooled")
        f_h, f_gelu, f_o, f_ob, f_ot, f_obs, f_y = (sem("f_h"), sem("f_gelu"), sem("f_o"), sem("f_ob"),
                                                    sem("f_ot"), sem("f_obs"), sem("f_y"))
        f_one = sem("f_one")
        d_val, d_vals, d_vst, d_om, d_oma, d_omv, d_omst, d_dxy = (
            sem("d_val"), sem("d_vals"), sem("d_vst"), sem("d_om"), sem("d_oma"), sem("d_omv"), sem("d_omst"),
            sem("d_dxy"))
        d_short, d_ext, d_all, d_rng, d_cmp = sem("d_short"), sem("d_ext"), sem("d_all"), sem("d_rng"), sem("d_cmp")
        hat_abs, hx_ready, hx_free, ay_ready, ay_free, ay_masked = (
            sem("hat_abs"), sem("hx_ready"), sem("hx_free"), sem("ay_ready"), sem("ay_free"), sem("ay_masked"))
        v_loaded, v_free = [sem("v_loaded0"), sem("v_loaded1")], [sem("v_free0"), sem("v_free1")]
        p_mult, p_ready, w_sum, m_ready, acc_sum = (sem("p_mult"), sem("p_ready"), sem("w_sum"), sem("m_ready"),
                                                    sem("acc_sum"))
        z_bank, acc_zero = sem("z_bank"), sem("acc_zero")
        d_smp, d_smst, d_smld, d_shld, d_wo, d_st, d_agg, d_mean, d_dev, d_varm = (
            sem("d_smp"), sem("d_smst"), sem("d_smld"), sem("d_shld"), sem("d_wo"), sem("d_st"), sem("d_agg"),
            sem("d_mean"), sem("d_dev"), sem("d_varm"))
        d_std, d_sc, d_bn, d_zs, d_wc = sem("d_std"), sem("d_sc"), sem("d_bn"), sem("d_zs"), sem("d_wc")
        stored = sem("stored")

        def bank(t, q):
            return t[:, q * BANK:(q + 1) * BANK]

        def inner(t, n, y0, ny, step=1, dx=0, w=None, r0=0, r1=128):
            w = w or t.shape[3] - 2
            nn = slice(0, NI) if n is None else slice(n, n + 1)
            return t[r0:r1, nn, y0:y0 + (ny - 1) * step + 1:step, dx:dx + (w - 1) * step + 1:step]

        CONVS = [("e0b0c1", A[0], A[1], None, None, 64), ("e0b0c2", A[1], A[2], A[0], None, 64),
                 ("e0b1c1", A[2], A[1], None, None, 64), ("e0b1c2", A[1], A[0], A[2], None, 64),
                 ("e1b0c1", A[0], B[0], None, None, 32), ("e1b0c2", B[0], B[1], None, A[0], 32),
                 ("e1b1c1", B[1], B[0], None, None, 32), ("e1b1c2", B[0], B[2], B[1], None, 32),
                 ("e2b0c1", B[2], D[0], None, None, 16), ("e2b0c2", D[0], D[1], None, B[2], 16),
                 ("e2b1c1", D[1], D[0], None, None, 16), ("e2b1c2", D[0], D[2], D[1], None, 16)]
        CHUNKS = []
        counts = {"act": 0, "dve": 0}
        FIRST_CHUNK = []
        for i, cv in enumerate(CONVS):
            FIRST_CHUNK.append(len(CHUNKS))
            for q in range(NQ if cv[5] == 64 else 1):
                who = "dve" if cv[3] is not None else "act"
                counts[who] += 1
                CHUNKS.append((i, q, who, counts[who]))

        def chunk_out(eng, j):
            _, _, who, n = CHUNKS[j]
            eng.wait_ge(evac_act if who == "act" else evac_dve, n)

        def source_chunks(i, q):
            if i == 0:
                return None
            n = FIRST_CHUNK[i] - FIRST_CHUNK[i - 1]
            return FIRST_CHUNK[i - 1] + ((1 if q < 2 else 3) if n == NQ and CONVS[i][5] == 64 else n - 1)

        def chunk_view(size, q):
            return (q // 2, q % 2 * 8, 8) if size == 64 else (None, 0, size // R)

        def psum_view(j, size):
            n, y0, ny = chunk_view(size, CHUNKS[j][1])
            cols = (1 if n is not None else NI) * ny * size
            return bank(psA, j % NQ)[:, 0:cols].rearrange(
                "p (n y x) -> p n y x", n=1 if n is not None else NI, y=ny)

        T3 = Tw.rearrange("p (v k m) -> p v k m", v=len(S1), k=3)
        S3 = Sw.rearrange("p (v b k m) -> p v b k m", v=2, b=2, k=3)
        E3 = Ew.rearrange("p (v b m) -> p v b m", v=2, b=2)
        D3 = Dw.rearrange("p (v h l m) -> p v h l m", v=2, h=2, l=2)
        raw3 = raw[:, 0:RAW3].rearrange("p (v k e o) -> p v k e o", v=12, k=3, e=3)
        raw_ds = raw[:, RAW3:RAW3 + 64].rearrange("p (v o) -> p v o", v=2)
        raw_up = raw[:, RAW3 + 64:RAWN].rearrange("p (v l m) -> p v l m", v=2, l=2)

        block = ctx.enter_context(nc.Block())

        def dcn_load_tiles(sp, l):
            sp.wait_ge(d_vals, NQ * (l + 1))
            if l == 0:
                sp.wait_ge(planes_zero, 16)
            for n in range(NI):
                for g in range(G):
                    at = (n * G + g) * PLANE - YS0 * CG * PCOLS - X0
                    dst = bass.AP(planes.tensor, at, [[PCOLS, 32], [R * CG * PCOLS, NY], [1, HW]])
                    sp.dma_start(dst, VAL[32 * g:32 * g + 32, n * 1024:(n + 1) * 1024].rearrange(
                        "p (y x) -> p y x", x=HW)).then_inc(d_vst, 16)
            sp.wait_ge(d_oma, 8 * (l + 1))
            sp.wait_ge(d_omv, 8 * (l + 1))
            for n in range(NI):
                sp.dma_start(om_dram[:, n], OMs[:, n].rearrange("p y r x -> p y (r x)")).then_inc(d_omst, 16)
            sp.wait_ge(d_omst, 32 * (l + 1))
            if l == 0:
                sp.wait_ge(f_y, NQ)
            for ng in range(NI * G):
                n, g = divmod(ng, G)
                src = om_dram[g * 27:(g + 1) * 27, n].rearrange("j y t -> y j t")
                sp.dma_start(dxy[16 * ng:16 * ng + 16, :].rearrange("p (j t) -> p j t", j=27), src)\
                    .then_inc(d_dxy, 16)

        def load_ffn(sp, f):
            if f == 1:
                sp.wait_ge(d_smp, 2 * NQ)
            sp.dma_start(W1s, w1[f].rearrange("e d h -> d e h")).then_inc(ffn_in, 16)
            sp.dma_start(W2s, w2[f, :, 0:HID].rearrange("e h o -> h e o")).then_inc(ffn_in, 16)
            sp.dma_start(W2b, w2b[f]).then_inc(ffn_in, 16)
            sp.dma_start(gb, bass.AP(gate_b.tensor, f * EXP, [[0, 8], [1, EXP], [1, 1]])).then_inc(ffn_in, 16)
            for r in range(R):
                sp.dma_start(graw[32 * r:32 * r + 32, :], gate_w[f]).then_inc(ffn_in, 16)

        FFN_IN = 16 * (4 + R)

        def walk(eng, pairs, chunks, body, chunk_start=None, chunk_end=None):
            xlo = eng.value_load(ranges[0:1, 0:1], min_val=0, max_val=NXC - 1)
            xhi = eng.value_load(ranges[0:1, 1:2], min_val=1, max_val=NXC)
            ylo = eng.value_load(ranges[0:1, 2:3], min_val=0, max_val=NYP - 1)
            yhi = eng.value_load(ranges[0:1, 3:4], min_val=1, max_val=NYP)
            with eng.Fori(xlo, xhi) as cx:
                nch = eng.snap(chunks)
                if chunk_start is not None:
                    chunk_start(cx, nch)
                with eng.Fori(ylo, yhi) as iy:
                    body(cx, iy, nch, eng.snap(pairs))
                    eng.reg_add(pairs, pairs, 1)
                if chunk_end is not None:
                    chunk_end()
                eng.reg_add(chunks, chunks, 1)
            return eng.snap(pairs)

        def counters(eng):
            regs = []
            for name in ("pairs_run", "chunks_run"):
                reg = eng.alloc_register(name)
                eng.reg_mov(reg, 0)
                regs.append(reg)
            return regs

        @block.sync
        def _(sp):
            sp.dma_start(cst[:, :], consts).then_inc(cst_in, 16)
            for n in range(NI):
                for r in range(R):
                    src = bass.AP(x.tensor, n * C * HW * HW + r * HW, [[HW * HW, C], [R * HW, NY], [1, HW]])
                    sp.dma_start(X[32 * r:32 * r + 32, n * 1024:(n + 1) * 1024].rearrange(
                        "p (y x) -> p y x", x=HW), src).then_inc(x_in, 16)
            for r in range(R):
                rows = slice(32 * r, 32 * r + 32)
                sp.dma_start(raw1[rows, 0, :], wv).then_inc(small_in, 16)
                sp.dma_start(raw1[rows, 1, :], bass.AP(wo.tensor, r * CG * C, [[0, 4], [C, CG], [1, C]]))\
                    .then_inc(small_in, 16)
                sp.dma_start(raw1[rows, 2, :], wct).then_inc(small_in, 16)
                sp.dma_start(Wom_r[rows, :], wom).then_inc(small_in, 16)
            for g in range(G):
                sp.dma_start(vecs[32 * g:32 * g + 32, 0:1], bass.AP(bv.tensor, g * CG, [[0, R], [1, CG], [1, 1]]))\
                    .then_inc(small_in, 16)
            sp.dma_start(vecs[:, 1:2], bass.AP(gamma.tensor, 0, [[0, R], [1, C], [1, 1]])).then_inc(small_in, 16)
            sp.dma_start(vecs[:, 2:3], bass.AP(beta.tensor, 0, [[0, R], [1, C], [1, 1]])).then_inc(small_in, 16)
            sp.dma_start(vecs[0:108, 3:4], bass.AP(bom.tensor, 0, [[1, 108], [1, 1]])).then_inc(small_in, 16)
            load_ffn(sp, 0)

            pairs, chunks = counters(sp)
            for l in range(2):
                if l == 0:
                    sp.wait_ge(ln_out, 3 * NQ)
                    sp.dma_start(short_dram, U).then_inc(d_short, 16)
                dcn_load_tiles(sp, l)
                sp.wait_ge(d_vst, 128 * (l + 1))
                sp.wait_ge(d_rng, l + 1)
                sp.wait_ge(acc_zero, NQ * (l + 1))

                def load_bands(cx, iy, nch, done):
                    for h in range(2):
                        sp.wait_ge(v_free[h], done + 1)
                        for ng in range(NI * G):
                            src = bass.AP(planes.tensor, (iy * 2 + h) * (CG * PCOLS) + cx * XC + ng * PLANE,
                                          [[R * CG * PCOLS, NY], [PCOLS, R * CG], [1, WB]])
                            sp.dma_start(Vt[16 * ng:16 * ng + 16, h], src).then_inc(v_loaded[h], 16)

                walk(sp, pairs, chunks, load_bands)
                sp.wait_ge(d_smp, NQ * (l + 1))
                sp.dma_start(smp_dram, SMP).then_inc(d_smst, 16)
                sp.wait_ge(d_smst, 16 * (l + 1))
                for ng in range(NI * G):
                    n, g = divmod(ng, G)
                    src = bass.AP(smp_dram.tensor, ng * NY * 2048, [[HW, 32], [2048, NY], [1, HW]])
                    sp.dma_start(VAL[32 * g:32 * g + 32, n * 1024:(n + 1) * 1024].rearrange(
                        "p (y x) -> p y x", x=HW), src).then_inc(d_smld, 16)
                if l == 1:
                    sp.dma_start(SHT, short_dram).then_inc(d_shld, 16)
            load_ffn(sp, 1)
            for q in range(NQ):
                sp.wait_ge(x_upd, 3 * NQ + q + 1)
                n, half = divmod(q, 2)
                for r in range(R):
                    dst = bass.AP(out.tensor, n * C * HW * HW + half * 8 * R * HW + r * HW,
                                  [[HW * HW, C], [R * HW, 8], [1, HW]])
                    sp.dma_start(dst, bank(X, q)[32 * r:32 * r + 32, :].rearrange("p (y x) -> p y x", x=HW))\
                        .then_inc(stored, 16)
            sp.wait_ge(stored, 16 * R * NQ)

        @block.gpsimd
        def _(pool):
            for r in range(R):
                pool.dma_start(raw[32 * r:32 * r + 32, :], convw).then_inc(raw_in, 16)
            pool.memset(Tw, 0.0).then_inc(w_zero, 1)
            pool.memset(area(7616, 2048), 0.0).then_inc(w_zero, 1)
            pool.memset(Dw, 0.0).then_inc(w_zero, 1)
            pool.wait_ge(w_zero, 3)
            pool.wait_ge(raw_in, 16 * R)
            made = [0]

            def copy(dst, src):
                if made[0]:
                    pool.wait_ge(w_ready, made[0])
                pool.tensor_copy(dst, src).then_inc(w_ready, 1)
                made[0] += 1

            for ro in range(R):
                for ky in range(3):
                    b, ri = divmod(2 * ro + ky - 1, R)
                    if b >= 0:
                        for v in range(2):
                            copy(S3[32 * ri:32 * ri + 32, v, b, :, 32 * ro:32 * ro + 32],
                                             raw3[32 * ri:32 * ri + 32, len(S1) + v, :, 2 - ky, :])
                b, ri = divmod(2 * ro, R)
                copy(E3[32 * ri:32 * ri + 32, :, b, 32 * ro:32 * ro + 32],
                                 raw_ds[32 * ri:32 * ri + 32, :, :])
            for ri in range(R):
                for v in range(2):
                    copy(D3[32 * ri:32 * ri + 32, v, ri // 2, :, (ri % 2) * 64:(ri % 2) * 64 + 64],
                                     raw_up[32 * ri:32 * ri + 32, v])
            pool.wait_ge(w_ready, made[0])
            pool.memset(zeros, 0.0).then_inc(zeroed, 1)
            pool.wait_ge(zeroed, 1)
            pool.dma_start(planes.rearrange("(p a w) -> p a w", p=128, a=4),
                           zeros.rearrange("p (a w) -> p a w", a=1).broadcast_to([128, 4, ZERO]))\
                .then_inc(planes_zero, 16)
            for l in range(2):
                pool.wait_ge(d_ext, 4 * (l + 1))
                pool.partition_all_reduce(small[:, 4:8], small[:, 0:4], 128, bass.bass_isa.ReduceOp.max)\
                    .then_inc(d_all, 1)
            pool.wait_ge(planes_zero, 16)

        W_ALL = 22 + 4 + 2 * R

        def banded_act(act):
            act.wait_ge(w_zero, 1)
            act.wait_ge(raw_in, 16 * R)
            for r in range(R):
                lo, hi = max(r - 1, 0), min(r + 2, R)
                src = raw3[32 * r:32 * r + 32, 0:len(S1), :, lo - r + 1:hi - r + 1, :]
                act.activation(T3[32 * r:32 * r + 32, :, :, 32 * lo:32 * hi].rearrange("p v k m -> p (v k) m"),
                               src.rearrange("p v k e o -> p (v k) (e o)"), ACT.Copy).then_inc(t_ready, 1)

        def ln_pe(pe, i, src, ready):
            for q in range(NQ):
                ready(pe, q)
                pe.matmul(bank(psA, q), const("chan_mean"), bank(src, q), start=True, stop=True)\
                    .then_inc(ln_mean, 1)
            for q in range(NQ):
                pe.wait_ge(ln_sq, NQ * i + q + 1)
                pe.matmul(bank(psA, q), const("chan_mean"), bank(SQ, q), start=True, stop=True)\
                    .then_inc(ln_var, 1)

        def ln_act(act, i, eps):
            for q in range(NQ):
                act.wait_ge(ln_cent, NQ * i + q + 1)
                act.activation(bank(SQ, q), bank(XCt, q), ACT.Square).then_inc(ln_sq, 1)
            for q in range(NQ):
                act.wait_ge(ln_var, NQ * i + q + 1)
                act.activation(bank(SQ, q), bank(psA, q), ACT.Sqrt, bias=const(eps)).then_inc(ln_std, 1)

        def ln_dve(dve, i, src, ready, dst):
            for q in range(NQ):
                ready(dve, q)
                dve.wait_ge(ln_mean, NQ * i + q + 1)
                dve.tensor_tensor(bank(XCt, q), bank(src, q), bank(psA, q), ALU.subtract).then_inc(ln_cent, 1)
            for q in range(NQ):
                dve.wait_ge(ln_std, NQ * i + q + 1)
                dve.reciprocal(bank(SQ, q), bank(SQ, q)).then_inc(ln_rstd, 1)
                dve.wait_ge(ln_rstd, NQ * i + q + 1)
                o, a, b = dst(q), bank(XCt, q), bank(SQ, q)
                if len(o.shape) == 3:
                    a, b = (t.rearrange("p (y x) -> p y x", x=HW) for t in (a, b))
                dve.tensor_tensor(o, a, b, ALU.mult).then_inc(ln_out, 1)

        def x_loaded(eng, q):
            if q == 0:
                eng.wait_ge(x_in, 16 * NI * R)

        def x_updated(stage):
            return lambda eng, q: eng.wait_ge(x_upd, NQ * stage + q + 1)

        def unet_pe(pe):
            pe.wait_ge(t_ready, R)
            pe.wait_ge(raw_in, 16 * R)
            pe.wait_ge(borders, 18)
            for j, (i, q, _, _) in enumerate(CHUNKS):
                name, src, _, _, ds_src, size = CONVS[i]
                if i == 0:
                    pe.wait_ge(ln_out, 2 if q < 2 else 4)
                else:
                    chunk_out(pe, source_chunks(i, q))
                if j >= NQ:
                    chunk_out(pe, j - NQ)
                n, y0, ny = chunk_view(size, q)
                ps = psum_view(j, size)
                if name in S1:
                    v, first = S1.index(name), True
                    for k in range(3):
                        pe.matmul(ps, T3[:, v, k, :], inner(src, n, y0 + 1, ny, 1, k), start=first, stop=False,
                                  skip_group_check=True)
                        first = False
                    for k in range(3):
                        pe.matmul(ps[0:32], raw3[96:128, v, k, 2, :], inner(src, n, y0, ny, 1, k, r0=96),
                                  start=False, stop=False, skip_group_check=True, tile_position=(96, 0))
                        mm = pe.matmul(ps[96:128], raw3[0:32, v, k, 0, :],
                                       inner(src, n, y0 + 2, ny, 1, k, r1=32), start=False, stop=True,
                                       skip_group_check=True, tile_position=(0, 96))
                    if ds_src is not None:
                        pe.wait_ge(w_ready, W_ALL)
                        u = 0 if size == 32 else 1
                        for b in range(2):
                            mm = pe.matmul(ps, E3[:, u, b, :], inner(ds_src, n, 1 + b, ny, 2, 1, size),
                                           start=False, stop=True, skip_group_check=True)
                else:
                    pe.wait_ge(w_ready, W_ALL)
                    v = S2.index(name)
                    for b in range(2):
                        for k in range(3):
                            pe.matmul(ps, S3[:, v, b, k, :], inner(src, n, 1 + b, ny, 2, k, size),
                                      start=b == 0 and k == 0, stop=False, skip_group_check=True)
                    for k in range(3):
                        mm = pe.matmul(ps[0:32], raw3[96:128, len(S1) + v, k, 2, :],
                                       inner(src, n, 0, ny, 2, k, size, r0=96), start=False, stop=True,
                                       skip_group_check=True, tile_position=(96, 0))
                mm.then_inc(conv_sum, 1)
            chunk_out(pe, len(CHUNKS) - 1)
            for h in range(2):
                for l in range(2):
                    o = bank(psA, 0).rearrange("p (n y a x b) -> p n y a x b", n=NI, y=4, a=2, b=2)[:, :, :, h, :, l]
                    for n in range(NI):
                        mm = pe.matmul(o[:, n], D3[:, 0, h, l, :], inner(D[2], n, 1, 4, 1, 1)[:, 0],
                                       start=True, stop=True, skip_group_check=True)
            mm.then_inc(up_sum, 1)
            pe.wait_ge(up_mix, 1)
            for q in range(NQ):
                n, half = divmod(q, 2)
                for h in range(2):
                    for l in range(2):
                        o = bank(psA, q).rearrange("p (y a x b) -> p y a x b", y=4, a=2, b=2)[:, :, h, :, l]
                        mm = pe.matmul(o, D3[:, 1, h, l, :], inner(B[0], n, 1 + 4 * half, 4, 1, 1)[:, 0],
                                       start=True, stop=True, skip_group_check=True)
                mm.then_inc(up_sum, 1)

        def unet_act(act):
            for j, (i, q, who, _) in enumerate(CHUNKS):
                if who != "act":
                    continue
                _, _, dst, _, _, size = CONVS[i]
                n, y0, ny = chunk_view(size, q)
                act.wait_ge(conv_sum, j + 1)
                act.activation(inner(dst, n, y0 + 1, ny, 1, 1), psum_view(j, size), ACT.Relu, scale=BN_S)\
                    .then_inc(evac_act, 1)
            act.wait_ge(up_sum, 1)
            act.activation(bank(up, 0), bank(psA, 0), ACT.Relu, scale=BN_S * BN_S).then_inc(up_relu, 1)
            for q in range(NQ):
                act.wait_ge(up_sum, q + 2)
                if q == 0:
                    act.wait_ge(up_mix, 1)
                act.activation(bank(up, q), bank(psA, q), ACT.Relu, scale=BN_S * BN_S).then_inc(up_relu, 1)

        def unet_dve(dve):
            done = 0
            for j, (i, q, who, _) in enumerate(CHUNKS):
                if who != "dve":
                    continue
                _, _, dst, res, _, size = CONVS[i]
                n, y0, ny = chunk_view(size, q)
                o, rr, ps = inner(dst, n, y0 + 1, ny, 1, 1), inner(res, n, y0 + 1, ny, 1, 1), psum_view(j, size)
                dve.wait_ge(conv_sum, j + 1)
                if i == 1:
                    dve.wait_ge(ln_out, NQ)
                if done:
                    dve.wait_ge(evac_dve, done)
                if size < 64:
                    chunk_out(dve, FIRST_CHUNK[i] - 2)
                for m in range(o.shape[1]):
                    ins = dve.scalar_tensor_tensor(out=o[:, m], in0=ps[:, m], scalar=BN_S, in1=rr[:, m],
                                                   op0=ALU.mult, op1=ALU.add)
                ins.then_inc(conv_res, 1)
                done += 1
                dve.wait_ge(conv_res, done)
                dve.tensor_scalar(o, o, 0.0, None, ALU.max).then_inc(evac_dve, 1)
            dve.wait_ge(evac_dve, done)
            dve.wait_ge(up_relu, 1)
            for n in range(NI):
                o = inner(B[0], n, 1, 8, 1, 1)[:, 0]
                ins = dve.scalar_tensor_tensor(
                    out=o, in0=inner(B[2], n, 1, 8, 1, 1)[:, 0], scalar=BN_S,
                    in1=bank(up, 0)[:, n * 256:(n + 1) * 256].rearrange("p (y x) -> p y x", x=32),
                    op0=ALU.mult, op1=ALU.add)
            ins.then_inc(up_mix, 1)
            for q in range(NQ):
                n, half = divmod(q, 2)
                u3 = bank(up, q).rearrange("p (y x) -> p y x", x=HW)
                dve.wait_ge(up_relu, q + 2)
                dve.scalar_tensor_tensor(out=u3, in0=inner(A[0], n, 1 + 8 * half, 8, 1, 1)[:, 0], scalar=BN_S,
                                         in1=u3, op0=ALU.mult, op1=ALU.add).then_inc(up_mix, 1)
                dve.wait_ge(up_mix, q + 2)
                dve.tensor_tensor(bank(X, q), bank(X, q), bank(up, q), ALU.add).then_inc(x_upd, 1)

        top8 = FX[:, 0:8]
        spread = FX[:, 8:40]
        cand = FX[0:32, 40:72]
        best = FX[0:32, 72:80]
        cand_rest = FX[0:32, 80:112]
        pack = FX[0:32, 112:145]
        picked = FX[:, 145:177]
        keep = FX[:, 177:185]
        drop = FX[:, 185:193]
        nmax = FX[:, 193:194]
        chosen = FX[:, 194:202]
        esum = FX[:, 202:203]
        rden = FX[:, 203:204]
        pooled = FX[0:33, 204:236]
        hid = FX[:, 236:268]
        oexp = FX[0:32, 268:396]
        OB = FX[:, 396:460].rearrange("p (h o) -> p h o", h=2)

        def ffn_pe(pe, f):
            for j in range(16):
                pe.wait_ge(ln_out, NQ * (1 if f == 0 else 3) + j // 4 + 1)
                mm = pe.transpose(psA[:, 128 * j:128 * j + 128], U[:, 128 * j:128 * j + 128], ident)
                if j % 4 == 3:
                    mm.then_inc(f_xt, 1)
            pe.wait_ge(f_gw, 2 * f + 2)
            for b in range(2):
                for pr in range(4):
                    for r in range(R):
                        for h in range(2):
                            n, quarter = pr // 2, 2 * (pr % 2) + h
                            o = psW[32 * pr:32 * pr + 32, b, :].rearrange("p (y r x) -> p y r x", y=2, r=R)[:, :, r]
                            at = n * 1024 + (quarter * 4 + 2 * b) * HW
                            mm = pe.matmul(o, Gw[:, r, h, :],
                                           U[:, at:at + 128].rearrange("p (y x) -> p y x", x=HW),
                                           start=r == 0 and h == 0, stop=r == 3 and h == 1,
                                           skip_group_check=True, tile_position=(0, 32 * pr))
                mm.then_inc(f_lg, 1)
            pe.wait_ge(f_ex, f + 1)
            pe.matmul(T0[0:32, 0:32], const("to_expert"), spread, start=True, stop=True).then_inc(f_cand, 1)
            pe.wait_ge(f_pack, 2 * f + 2)
            pe.matmul(T1[:, 0:33], const("from_expert", 32), pack, start=True, stop=True).then_inc(f_back, 1)
            pe.wait_ge(f_exp, f + 1)
            pe.matmul(T0[:, 0:1], const("same_expert"), esum, start=True, stop=True).then_inc(f_den, 1)
            for j in range(8):
                pe.wait_ge(f_p, 2 * f + j // 4 + 1)
                mm = pe.transpose(psW[:, j // 4, 128 * (j % 4):128 * (j % 4) + 128], Pm[:, 128 * j:128 * j + 128],
                                  ident)
                if j % 4 == 3:
                    mm.then_inc(f_pt, 1)
            pe.wait_ge(f_xts, NQ * (f + 1))
            pe.wait_ge(f_pts, 2 * (f + 1))
            for n in range(NI):
                for quarter in range(4):
                    for b in range(2):
                        for r in range(R):
                            at = n * 64 + quarter * 16
                            mm = pe.matmul(T1[0:32, n * 16:n * 16 + 16],
                                           XTs[:, n * 8 + quarter * 2 + b, 32 * r:32 * r + 32],
                                           PTs[:, 4 * b + r, at:at + 16],
                                           start=n == quarter == b == r == 0, stop=quarter == 3 and b == 1 and r == 3,
                                           skip_group_check=True)
            mm.then_inc(f_pool, 1)
            pe.wait_ge(f_pooled, f + 1)
            for e in range(EXP):
                mm = pe.matmul(T0[:, 2 * e:2 * e + 2], W1s[:, e, :], pooled[:, e:e + 17:16], start=True, stop=True,
                               skip_group_check=True)
            mm.then_inc(f_h, 1)
            pe.wait_ge(f_gelu, f + 1)
            for e in range(EXP):
                mm = pe.matmul(T1[0:32, 2 * e:2 * e + 2], W2s[:, e, :], hid[:, 2 * e:2 * e + 2], start=True,
                               stop=True, skip_group_check=True)
            mm.then_inc(f_o, 1)
            pe.wait_ge(f_ob, f + 1)
            pe.transpose(T0[:, 0:32], oexp, ident[0:32, 0:32]).then_inc(f_ot, 1)
            pe.wait_ge(f_obs, f + 1)
            for q in range(NQ):
                for h in range(2):
                    for r in range(R):
                        o = psA[32 * r:32 * r + 32, q * BANK + h * 256:q * BANK + h * 256 + 256]
                        mm = pe.matmul(o.rearrange("p (b t) -> p b t", b=2), OB[32 * q:32 * q + 32, h, :],
                                       Pm[32 * q:32 * q + 32, :].rearrange("p (b r t) -> p b r t", b=2, r=R)[:, :, r],
                                       start=True, stop=True, skip_group_check=True,
                                       tile_position=(32 * q, 32 * r))
                mm.then_inc(f_y, 1)

        def ffn_act(act, f):
            if f == 0:
                act.wait_ge(planes_zero, 16)
            for q in range(NQ):
                act.wait_ge(f_xt, NQ * f + q + 1)
                act.activation(XTs[:, 4 * q:4 * q + 4, :].rearrange("p j m -> p (j m)"), bank(psA, q), ACT.Copy)\
                    .then_inc(f_xts, 1)
            act.wait_ge(f_max, f + 1)
            act.activation(Ee, LG[:, 0:TOK], ACT.Exp, bias=nmax, accum_out=esum).then_inc(f_exp, 1)
            act.wait_ge(f_rest, f + 1)
            act.activation(E2, LGr[:, 0:TOK], ACT.Exp, bias=nmax).then_inc(f_exp2, 1)
            for b in range(2):
                act.wait_ge(f_pt, 2 * f + b + 1)
                act.activation(PTs[:, 4 * b:4 * b + 4, :].rearrange("p j m -> p (j m)"), psW[:, b, :], ACT.Copy)\
                    .then_inc(f_pts, 1)
            act.wait_ge(f_h, f + 1)
            act.activation(hid, T0[:, 0:32], ACT.Gelu).then_inc(f_gelu, 1)

        def ffn_dve(dve, f):
            if f == 0:
                dve.wait_ge(planes_zero, 16)
            dve.wait_ge(ffn_in, FFN_IN * (f + 1))
            dve.tensor_tensor(Gh.rearrange("p h (a e) -> p h a e", a=2),
                              graw.rearrange("p (h a e) -> p h a e", h=1, a=1).broadcast_to([128, 2, 2, EXP]),
                              const("half").rearrange("p (h a e) -> p h a e", h=2, e=1).broadcast_to(
                                  [128, 2, 2, EXP]), ALU.mult).then_inc(f_gw, 1)
            dve.wait_ge(f_gw, 2 * f + 1)
            dve.tensor_tensor(Gw.rearrange("p r h j -> p r (h j)"),
                              Gh.rearrange("p (o h) j -> p o (h j)", o=1).broadcast_to([128, R, 64]),
                              const("rowsel").rearrange("p (r o) -> p r o", o=1).broadcast_to([128, R, 64]),
                              ALU.mult).then_inc(f_gw, 1)
            dve.memset(LG[:, TOK:TOK + 8], LOW).then_inc(f_one, 1)
            dve.memset(pooled[32:33, :], 1.0).then_inc(f_one, 1)
            for b in range(2):
                dve.wait_ge(f_lg, 2 * f + b + 1)
                dve.tensor_scalar(LG[:, b * BANK:(b + 1) * BANK], psW[:, b, :], gb, None, ALU.add).then_inc(f_lgs, 1)
            dve.wait_ge(f_lgs, 2 * f + 2)
            dve.wait_ge(f_one, 2 * f + 2)
            dve.max(top8, LG[:, 0:TOK]).then_inc(f_top, 1)
            dve.wait_ge(f_top, f + 1)
            dve.tensor_tensor(spread.rearrange("p (q j) -> p q j", q=4),
                              top8.rearrange("p (q j) -> p q j", q=1).broadcast_to([128, 4, 8]),
                              const("quarter").rearrange("p (q j) -> p q j", j=1).broadcast_to([128, 4, 8]),
                              ALU.mult).then_inc(f_ex, 1)
            dve.wait_ge(f_cand, f + 1)
            dve.tensor_copy(cand, T0[0:32, 0:32]).then_inc(f_ct, 1)
            dve.wait_ge(f_ct, 3 * f + 1)
            dve.max(best, cand).then_inc(f_ct, 1)
            dve.wait_ge(f_ct, 3 * f + 2)
            dve.match_replace(cand_rest, best, cand, LOW).then_inc(f_ct, 1)
            dve.tensor_copy(pack[:, 32:33], best[:, 0:1]).then_inc(f_pack, 1)
            dve.wait_ge(f_ct, 3 * f + 3)
            dve.tensor_tensor(pack[:, 0:32], cand, cand_rest, ALU.not_equal).then_inc(f_pack, 1)
            dve.wait_ge(f_back, f + 1)
            dve.tensor_scalar(nmax, T1[:, 32:33], -1.0, None, ALU.mult).then_inc(f_max, 1)
            dve.tensor_tensor(picked.rearrange("p (q j) -> p q j", q=4),
                              T1[:, 0:32].rearrange("p (q j) -> p q j", q=4),
                              const("quarter").rearrange("p (q j) -> p q j", j=1).broadcast_to([128, 4, 8]),
                              ALU.mult).then_inc(f_msk, 1)
            dve.wait_ge(f_msk, 4 * f + 1)
            dve.tensor_reduce(keep, picked.rearrange("p (q j) -> p j q", q=4), AX_X, ALU.add).then_inc(f_msk, 1)
            dve.wait_ge(f_msk, 4 * f + 2)
            dve.tensor_scalar(drop, keep, -1.0, -LOW, ALU.add, ALU.mult).then_inc(f_msk, 1)
            dve.tensor_tensor(chosen, keep, top8, ALU.mult).then_inc(f_msk, 1)
            dve.wait_ge(f_msk, 4 * f + 4)
            dve.tensor_tensor(chosen, chosen, drop, ALU.add).then_inc(f_rden, 1)
            dve.wait_ge(f_rden, 2 * f + 1)
            dve.match_replace(LGr, chosen, LG, LOW).then_inc(f_rest, 1)
            dve.wait_ge(f_den, f + 1)
            dve.reciprocal(rden, T0[:, 0:1]).then_inc(f_rden, 1)
            dve.wait_ge(f_exp2, f + 1)
            for b in range(2):
                o = Pm[:, b * BANK:(b + 1) * BANK].rearrange("p (r y x) -> p r y x", r=R, y=2)
                s = [t[:, b * BANK:(b + 1) * BANK].rearrange("p (y r x) -> p r y x", y=2, r=R) for t in (Ee, E2)]
                dve.tensor_tensor(o, s[0], s[1], ALU.subtract).then_inc(f_dif, 1)
            dve.wait_ge(f_rden, 2 * f + 2)
            for b in range(2):
                dve.wait_ge(f_dif, 2 * f + b + 1)
                o = Pm[:, b * BANK:(b + 1) * BANK]
                dve.tensor_scalar(o, o, rden, None, ALU.mult).then_inc(f_p, 1)
            dve.wait_ge(f_pool, f + 1)
            dve.tensor_copy(pooled[0:32, :], T1[0:32, 0:32]).then_inc(f_pooled, 1)
            dve.wait_ge(f_o, f + 1)
            o = oexp.rearrange("p (n q e) -> p n q e", n=NI, q=4)
            for n in range(NI):
                ins = dve.tensor_tensor(
                    o[:, n], T1[0:32, 0:32].rearrange("p (e n) -> p n e", n=NI)[:, n:n + 1].broadcast_to([32, 4, EXP]),
                    W2b.rearrange("p (q e) -> p q e", q=1).broadcast_to([32, 4, EXP]), ALU.add)
            ins.then_inc(f_ob, 1)
            dve.wait_ge(f_ot, f + 1)
            for h in range(2):
                ins = dve.tensor_scalar(OB[:, h, :], T0[:, 0:32], const("parity")[:, h:h + 1], None, ALU.mult)
            ins.then_inc(f_obs, 1)
            for q in range(NQ):
                dve.wait_ge(f_y, NQ * f + q + 1)
                dve.tensor_tensor(bank(X, q), bank(X, q), bank(psA, q), ALU.add).then_inc(x_upd, 1)

        def dcn_pe(pe, l, pairs, chunks):
            src = U if l == 0 else T2
            for q in range(NQ):
                if l == 0:
                    pe.wait_ge(ln_out, 2 * NQ + q + 1)
                else:
                    pe.wait_ge(d_bn, q + 1)
                if q == 0:
                    pe.wait_ge(bd_ready, 4)
                pe.matmul(bank(psA, q), Wv_bd[:, :], bank(src, q), start=True, stop=True).then_inc(d_val, 1)
            for r in range(R):
                for q in range(NQ):
                    k = r * NQ + q
                    if k >= 4:
                        pe.wait_ge(d_oma if k % 2 == 0 else d_omv, 8 * l + k // 2 - 1)
                    pe.matmul([psW[:, 0], psW[:, 1], T0, T1][k % 4][0:108, :], Wom_r[32 * r:32 * r + 32, :],
                              bank(src, q)[32 * r:32 * r + 32, :], start=True, stop=True,
                              tile_position=(32 * r, 0)).then_inc(d_om, 1)
            pe.wait_ge(z_bank, l + 1)
            pe.wait_ge(d_vals, NQ * (l + 1))
            pe.wait_ge(d_oma, 8 * (l + 1))
            pe.wait_ge(d_omv, 8 * (l + 1))
            for q in range(NQ):
                pe.matmul(bank(psA, q), ident, zero_bank, start=True, stop=True, skip_group_check=True)\
                    .then_inc(acc_zero, 1)
            pe.wait_ge(d_rng, l + 1)

            def sums(cx, iy, nch, done):
                for s in range(STEPS + 1):
                    if s < STEPS:
                        pe.wait_ge(p_ready, done * STEPS + (s + 1))
                        for k in range(FOLD, K):
                            mm = pe.matmul(psW[:, s % 2, 0:256], ident, Pt[:, s % 2, k * 256:(k + 1) * 256],
                                           start=k == FOLD, stop=k == K - 1, skip_group_check=True)
                        mm.then_inc(w_sum, 1)
                    if s > 0:
                        t = s - 1
                        pe.wait_ge(m_ready, done * STEPS + (t + 1))
                        for q in range(NQ):
                            mm = pe.matmul(bank(psA, q), ident, bank(Mt[:, t % 2], q), start=False, stop=True,
                                           skip_group_check=True)
                        mm.then_inc(acc_sum, 1)

            walk(pe, pairs, chunks, sums)
            for q in range(NQ):
                if q == 0:
                    pe.wait_ge(d_smld, 128 * (l + 1))
                    pe.wait_ge(d_smp, NQ * (l + 1))
                pe.matmul(bank(psA, q), Wo_bd[:, :], bank(VAL, q), start=True, stop=True).then_inc(d_wo, 1)
            pe.wait_ge(d_agg, l + 1)
            pe.matmul(T0[:, 0:1], const("row_mean"), small[:, 8:9], start=True, stop=True).then_inc(d_mean, 1)
            pe.wait_ge(d_dev, 3 * l + 3)
            pe.matmul(T1[:, 0:1], const("row_mean"), small[:, 10:11], start=True, stop=True).then_inc(d_varm, 1)
            if l == 1:
                for q in range(NQ):
                    pe.wait_ge(d_zs, q + 1)
                    pe.matmul(bank(psA, q), Wc_bd[:, :], bank(Zt, q), start=True, stop=True).then_inc(d_wc, 1)

        def dcn_act(act, l, pairs, chunks, abses):
            for q in range(NQ):
                act.wait_ge(d_val, NQ * l + q + 1)
                if l == 1 and q == 0:
                    act.wait_ge(d_wo, NQ)
                act.activation(bank(VAL, q), bank(psA, q), ACT.Identity, bias=vecs[:, 0:1]).then_inc(d_vals, 1)
            for k in range(0, R * NQ, 2):
                r, q = divmod(k, NQ)
                act.wait_ge(d_om, 16 * l + k + 1)
                if k == 0:
                    act.wait_ge(bd_ready, 4)
                act.activation(OMs[:, q // 2, q % 2 * 8:q % 2 * 8 + 8, r, :],
                               [psW[:, 0], psW[:, 1], T0, T1][k % 4][0:108, :].rearrange("p (y x) -> p y x", x=HW),
                               ACT.Identity, bias=vecs[0:108, 3:4]).then_inc(d_oma, 1)
            act.wait_ge(d_dxy, 128 * (l + 1))
            act.wait_ge(d_vst, 128 * (l + 1))
            act.wait_ge(d_short, 16)
            act.wait_ge(d_rng, l + 1)

            def hat(dst, src, shift, done):
                act.activation(dst, src, ACT.Abs, bias=shift).then_inc(hat_abs, 1)
                act.reg_add(abses, abses, 1)
                act.wait_ge(hat_abs, act.snap(abses))
                act.activation(dst, dst, ACT.Relu, bias=1.0, scale=-1.0).then_inc(done, 1)

            def column_hats(cx, nch):
                act.wait_ge(hx_free, nch + 1)
                for j in range(XC):
                    hat(hx[:, j, :], dx, const("xtab")[:, bass.ds(cx * XC + j, 1)], hx_ready)

            def row_hats(cx, iy, nch, done):
                for h in range(2):
                    act.wait_ge(ay_free, done * 2 + (h + 1))
                    hat(ay[:, h, :], dy, const("ytab")[:, bass.ds(iy * 2 + h, 1)], ay_ready)

            walk(act, pairs, chunks, row_hats, column_hats)
            act.wait_ge(d_varm, l + 1)
            act.wait_ge(d_dev, 3 * l + 3)
            act.activation(small[:, 11:12], T1[:, 0:1], ACT.Sqrt, bias=const("eps5")).then_inc(d_std, 1)
            act.wait_ge(d_sc, 4 * l + 4)
            for q in range(NQ):
                if l == 0:
                    act.activation(bank(T2, q), bank(psA, q), ACT.Relu, bias=small[:, 14:15],
                                   scale=small[:, 13:14]).then_inc(d_bn, 1)
                else:
                    act.activation(bank(Zt, q), bank(psA, q), ACT.Identity, bias=small[:, 14:15],
                                   scale=small[:, 13:14]).then_inc(d_bn, 1)

        def dcn_dve(dve, l, pairs, chunks):
            if l == 0:
                dve.wait_ge(small_in, 16 * (4 * R + G + 3))
                rs, cs = const("rowsel"), const("colsel")
                dve.tensor_tensor(Wv_bd[:, :].rearrange("p (g r c) -> p g r c", g=G, r=R),
                                  raw1[:, 0, :].rearrange("p (g r c) -> p g r c", g=G, r=1).broadcast_to(
                                      [128, G, R, CG]),
                                  rs.rearrange("p (g r c) -> p g r c", g=1, c=1).broadcast_to([128, G, R, CG]),
                                  ALU.mult).then_inc(bd_ready, 1)
                for w, i, s in ((Wo_bd, 1, cs), (Wc_bd, 2, rs)):
                    dve.tensor_tensor(w[:, :].rearrange("p (r c) -> p r c", r=R),
                                      raw1[:, i, :].rearrange("p (r c) -> p r c", r=1).broadcast_to([128, R, C]),
                                      s.rearrange("p (r c) -> p r c", c=1).broadcast_to([128, R, C]),
                                      ALU.mult).then_inc(bd_ready, 1)
                dve.tensor_tensor(vecs[0:108, 3:4], vecs[0:108, 3:4], const("tapoff", 108), ALU.add)\
                    .then_inc(bd_ready, 1)
                dve.wait_ge(bd_ready, 4)
            for k in range(1, R * NQ, 2):
                r, q = divmod(k, NQ)
                dve.wait_ge(d_om, 16 * l + k + 1)
                dve.tensor_scalar(OMs[:, q // 2, q % 2 * 8:q % 2 * 8 + 8, r, :],
                                  [psW[:, 0], psW[:, 1], T0, T1][k % 4][0:108, :].rearrange(
                                      "p (y x) -> p y x", x=HW),
                                  vecs[0:108, 3:4], None, ALU.add).then_inc(d_omv, 1)
            dve.memset(zero_bank, 0.0).then_inc(z_bank, 1)
            dve.wait_ge(d_dxy, 128 * (l + 1))
            for i, (t, op) in enumerate(((dx, ALU.min), (dx, ALU.max), (dy, ALU.min), (dy, ALU.max))):
                dve.tensor_reduce(small[:, i:i + 1], t, AX_X, op).then_inc(d_cmp, 1)
            dve.wait_ge(d_cmp, 16 * l + 4)
            for i in range(4):
                dve.tensor_scalar(small[:, i:i + 1], small[:, i:i + 1], -1.0 if i % 2 == 0 else 1.0, None,
                                  ALU.mult).then_inc(d_ext, 1)
            dve.wait_ge(d_all, l + 1)
            fr = area(47936 - 80, 80)[0:1, :]
            for i, (name, op) in enumerate((("xlow", ALU.is_ge), ("xhigh", ALU.is_lt), ("ylow", ALU.is_ge),
                                            ("yhigh", ALU.is_lt))):
                tab = const(name, 1)
                w = tab.shape[1]
                dve.tensor_scalar(fr[:, 0:w], tab, small[0:1, 4 + i:5 + i], None, op).then_inc(d_cmp, 1)
                dve.wait_ge(d_cmp, 16 * l + 5 + 3 * i)
                dve.tensor_reduce(fr[:, 70 + i:71 + i], fr[:, 0:w], AX_X, ALU.add).then_inc(d_cmp, 1)
                dve.wait_ge(d_cmp, 16 * l + 6 + 3 * i)
                n = NXC if i < 2 else NYP
                lo, hi = (0.0, n - 1.0) if i % 2 == 0 else (1.0, float(n))
                dve.tensor_scalar(fr[:, 74 + i:75 + i], fr[:, 70 + i:71 + i], lo, hi, ALU.max, ALU.min)\
                    .then_inc(d_cmp, 1)
                dve.wait_ge(d_cmp, 16 * l + 7 + 3 * i)
            dve.tensor_copy(ranges[:, :], fr[:, 74:78]).then_inc(d_rng, 1)
            dve.wait_ge(d_rng, l + 1)
            if l == 0:
                dve.sem_inc(v_free[0], 1)
                dve.sem_inc(v_free[1], 1)
                dve.sem_inc(hx_free, 1)
                dve.sem_inc(ay_free, 2)
                dve.sem_inc(acc_sum, 2)

            def weights(cx, iy, nch, done):
                def product(s):
                    h, j = divmod(s, XC)
                    if j == 0:
                        dve.wait_ge(ay_ready, done * 2 + (h + 1))
                        dve.tensor_tensor(ay[:, h, :], ay[:, h, :], mk, ALU.mult).then_inc(ay_masked, 1)
                        dve.wait_ge(ay_masked, done * 2 + (h + 1))
                    if h == 0:
                        dve.wait_ge(hx_ready, nch * XC + (j + 1))
                    if s >= 2:
                        dve.wait_ge(w_sum, done * STEPS + (s - 1))
                    dve.tensor_tensor(Pt[:, s % 2], ay[:, h, :], hx[:, j, :], ALU.mult).then_inc(p_mult, 1)
                    dve.wait_ge(p_mult, done * STEPS + (s + 1))
                    a, b = Pt[:, s % 2, 0:FOLD * 256], Pt[:, s % 2, FOLD * 256:2 * FOLD * 256]
                    dve.tensor_tensor(b, a, b, ALU.add).then_inc(p_ready, 1)

                def weigh(s):
                    h, j = divmod(s, XC)
                    dve.wait_ge(w_sum, done * STEPS + (s + 1))
                    if j == 0:
                        dve.wait_ge(v_loaded[h], done * 128 + 128)
                    dve.wait_ge(acc_sum, done * STEPS + (s + 1))
                    w = psW[:, s % 2, 0:256].rearrange("p (r o x) -> p r o x", r=R, o=1)
                    dve.tensor_tensor(Mt[:, s % 2].rearrange("p (r c x) -> p r c x", r=R, c=CG),
                                      Vt[:, h, :, j:j + HW].rearrange("p (r c) x -> p r c x", r=R),
                                      w.broadcast_to([128, R, CG, HW]), ALU.mult).then_inc(m_ready, 1)
                    if j == XC - 1:
                        dve.wait_ge(m_ready, done * STEPS + (s + 1))
                        dve.sem_inc(v_free[h], 1)
                        dve.sem_inc(ay_free, 1)

                for s in range(STEPS + 1):
                    if s < STEPS:
                        product(s)
                    if s > 0:
                        weigh(s - 1)

            done = walk(dve, pairs, chunks, weights, chunk_end=lambda: dve.sem_inc(hx_free, 1))
            dve.wait_ge(acc_sum, done * STEPS + 2)
            dve.wait_ge(p_ready, done * STEPS)
            for q in range(NQ):
                dve.tensor_copy(bank(SMP, q), bank(psA, q)).then_inc(d_smp, 1)
            for q in range(NQ):
                dve.wait_ge(d_wo, NQ * l + q + 1)
                dve.bn_stats(stats[:, q, :], bank(psA, q)).then_inc(d_st, 1)
            dve.wait_ge(d_st, NQ * (l + 1))
            dve.bn_aggr(small[:, 8:10], stats[:, :, :]).then_inc(d_agg, 1)
            dve.wait_ge(d_mean, l + 1)
            dve.tensor_tensor(small[:, 12:13], small[:, 8:9], T0[:, 0:1], ALU.subtract).then_inc(d_dev, 1)
            dve.wait_ge(d_dev, 3 * l + 1)
            dve.tensor_tensor(small[:, 12:13], small[:, 12:13], small[:, 12:13], ALU.mult).then_inc(d_dev, 1)
            dve.wait_ge(d_dev, 3 * l + 2)
            dve.wait_ge(d_agg, l + 1)
            dve.tensor_tensor(small[:, 10:11], small[:, 12:13], small[:, 9:10], ALU.add).then_inc(d_dev, 1)
            dve.wait_ge(d_std, l + 1)
            dve.reciprocal(small[:, 13:14], small[:, 11:12]).then_inc(d_sc, 1)
            dve.wait_ge(d_sc, 4 * l + 1)
            dve.tensor_tensor(small[:, 13:14], small[:, 13:14], vecs[:, 1:2], ALU.mult).then_inc(d_sc, 1)
            dve.wait_ge(d_sc, 4 * l + 2)
            dve.tensor_tensor(small[:, 15:16], T0[:, 0:1], small[:, 13:14], ALU.mult).then_inc(d_sc, 1)
            dve.wait_ge(d_sc, 4 * l + 3)
            dve.tensor_tensor(small[:, 14:15], vecs[:, 2:3], small[:, 15:16], ALU.subtract).then_inc(d_sc, 1)
            if l == 1:
                dve.wait_ge(d_shld, 16)
                for q in range(NQ):
                    dve.wait_ge(d_bn, NQ + q + 1)
                    dve.tensor_tensor(bank(Zt, q), bank(Zt, q), bank(SHT, q), ALU.add).then_inc(d_zs, 1)
                for q in range(NQ):
                    dve.wait_ge(d_wc, q + 1)
                    dve.tensor_tensor(bank(X, q), bank(X, q), bank(psA, q), ALU.add).then_inc(x_upd, 1)

        LN_FOR = [(0, x_loaded, "eps6"), (1, x_updated(0), "eps5"), (2, x_updated(1), "eps6"),
                  (3, x_updated(2), "eps5")]

        @block.tensor
        def _(pe):
            pe.wait_ge(cst_in, 16)
            pairs, chunks = counters(pe)
            ln_pe(pe, 0, X, x_loaded)
            unet_pe(pe)
            ln_pe(pe, 1, X, x_updated(0))
            ffn_pe(pe, 0)
            ln_pe(pe, 2, X, x_updated(1))
            for l in range(2):
                dcn_pe(pe, l, pairs, chunks)
            ln_pe(pe, 3, X, x_updated(2))
            ffn_pe(pe, 1)

        @block.scalar
        def _(act):
            act.wait_ge(cst_in, 16)
            pairs, chunks = counters(act)
            abses = act.alloc_register("abses_run")
            act.reg_mov(abses, 0)
            banded_act(act)
            ln_act(act, 0, "eps6")
            unet_act(act)
            ln_act(act, 1, "eps5")
            ffn_act(act, 0)
            ln_act(act, 2, "eps6")
            for l in range(2):
                dcn_act(act, l, pairs, chunks, abses)
            ln_act(act, 3, "eps5")
            ffn_act(act, 1)

        @block.vector
        def _(dve):
            dve.wait_ge(cst_in, 16)
            pairs, chunks = counters(dve)
            for t in A + B + D:
                ny, w = t.shape[2], t.shape[3]
                dve.memset(t[:, :, 0:ny:ny - 1, :], 0.0).then_inc(borders, 1)
                dve.memset(t[:, :, 1:ny - 1, 0:w:w - 1], 0.0).then_inc(borders, 1)
            ln_dve(dve, 0, X, x_loaded,
                   lambda q: inner(A[0], q // 2, 1 + q % 2 * 8, 8, 1, 1)[:, 0])
            unet_dve(dve)
            ln_dve(dve, 1, X, x_updated(0), lambda q: bank(U, q))
            ffn_dve(dve, 0)
            ln_dve(dve, 2, X, x_updated(1), lambda q: bank(U, q))
            for l in range(2):
                dcn_dve(dve, l, pairs, chunks)
            ln_dve(dve, 3, X, x_updated(2), lambda q: bank(U, q))
            ffn_dve(dve, 1)


def prepare(inputs):
    def a(name):
        return np.asarray(inputs[name])

    w3 = np.stack([a("L0_conv_" + n) for n in S1 + S2])
    w3 = w3.transpose(2, 0, 4, 3, 1)[:, :, :, ::-1, :].reshape(C, RAW3)
    ds = np.stack([a("L0_conv_" + n)[:, :, 0, 0] for n in DS]).transpose(2, 0, 1).reshape(C, 64)
    dec = np.stack([a("L0_conv_" + n) for n in DEC]).transpose(1, 0, 4, 3, 2).reshape(C, 256)
    wom = a("L1_conv_Wom").reshape(C, G, 27)
    bom = a("L1_conv_bom").reshape(1, G, 27)

    def planes(t):
        off = t[:, :, 0:18].reshape(-1, G, K, 2).transpose(0, 1, 3, 2).reshape(-1, G, 18)
        return np.concatenate([off, t[:, :, 18:27]], axis=2).reshape(-1, 108)

    arrays = {
        "x": a("x"),
        "convw": np.concatenate([w3, ds, dec], axis=1),
        "gate_w": np.stack([a(f"L{f}_ffn_gate_w").T for f in range(2)]),
        "gate_b": np.stack([a(f"L{f}_ffn_gate_b") for f in range(2)]),
        "w1": np.stack([a(f"L{f}_ffn_weight1") for f in range(2)]),
        "w2": np.stack([a(f"L{f}_ffn_weight2") for f in range(2)]),
        "w2b": np.stack([a(f"L{f}_ffn_weight2")[:, HID, :].T for f in range(2)]),
        "wv": a("L1_conv_Wv"),
        "bv": a("L1_conv_bv"),
        "wom": planes(wom),
        "bom": planes(bom)[0],
        "wo": a("L1_conv_Wo"),
        "gamma": a("L1_conv_gamma"),
        "beta": a("L1_conv_beta"),
        "wct": a("L1_conv_Wc").T,
        "consts": constants(),
    }
    return {k: np.ascontiguousarray(v) for k, v in arrays.items()}


def kernel(**inputs):
    import concourse.bacc as _bacc
    from concourse.bass_utils import run_bass_kernel_spmd as _run

    nc = _bacc.Bacc("TRN2", target_bir_lowering=False, num_devices=1)
    arrays, args = {}, []
    for name, a in prepare(inputs).items():
        arrays[f"in_{name}"] = a
        args.append(nc.dram_tensor(f"in_{name}", a.shape, mybir.dt.from_np(a.dtype), kind="ExternalInput").ap())
    out = nc.dram_tensor("out_x", (NI, C, HW, HW), F32, kind="ExternalOutput").ap()
    metaformer_kernel(nc, *args, out)
    return _run(nc, [arrays], core_ids=[0]).results[0]["out_x"]
```

```python
import itertools
from contextlib import ExitStack

import numpy as np

import concourse.bass as bass
from concourse import mybir

F32 = mybir.dt.float32
I32 = mybir.dt.int32
ALU = mybir.AluOpType
ACT = mybir.ActivationFunctionType
AX_X = mybir.AxisListType.X

NI, C, HW = 2, 32, 64
R = 4
NY = HW // R
COLS = NI * NY * HW
BANK = 512
NQ = COLS // BANK
EXP, TOPK, HID = 16, 8, 128
TOK = 1024
LOW = -3.0e38
FAR = -1.0e30
G, K, CG = 4, 9, 8
TAPS = K * R * HW

XC, NXC, X0 = 10, 13, -65
NYP, YS0 = 64, -64
XP = XC // 2
TRI = 3 * R * HW
PROWS = 2 * NYP + HW
PCOLS = XC * NXC + HW
WB = HW + XC - 1
PLANE = PROWS * CG * PCOLS
TAPS_FULL = (9, 1, (4,))
TAPS_TWO = (6, 0, (3, 1))
LEAD = 2
ZERO = NI * G * PLANE // (128 * 4)

BN_S = float(1.0 / np.sqrt(1.0 + 0.001))

S1 = ["e0b0c1", "e0b0c2", "e0b1c1", "e0b1c2", "e1b0c2", "e1b1c1", "e1b1c2", "e2b0c2", "e2b1c1", "e2b1c2"]
S2 = ["e1b0c1", "e2b0c1"]
DS = ["e1b0ds", "e2b0ds"]
DEC = ["dec0w", "dec1w"]
RAW3 = (len(S1) + len(S2)) * 288
RAWN = RAW3 + 2 * 32 + 2 * 128


def columns(*sizes):
    at, out = 0, {}
    for name, n in sizes:
        out[name] = (at, at + n)
        at += n
    return out, at


CONST, NCONST = columns(
    ("ident", 128), ("chan_mean", 128), ("chan_mean4", 4), ("eps6", 1), ("eps5", 1), ("row_mean", 128), ("same_expert", 128), ("to_expert", 32),
    ("from_expert", 128), ("quarter", 4), ("parity", 2), ("rowsel", 4), ("colsel", 4), ("half", 4),
    ("tapoff", 1), ("ytab", 2 * NYP), ("xtab", XC * NXC),
    ("yabove", 2 * NYP), ("ybelow", 2 * NYP), ("xabove", XP * NXC), ("xbelow", XP * NXC), ("taprow", 3),
    ("fromend", XP * NXC), ("fromstart", XP * NXC), ("notx", 1), ("noty", 1),
    ("xlow", NXC), ("xhigh", NXC))
FIRST_CONST = CONST["row_mean"][0]


def constants():
    t = np.zeros((128, NCONST), np.float32)

    def put(name, a):
        lo, hi = CONST[name]
        t[:a.shape[0], lo:hi] = a

    p = np.arange(128)
    put("ident", np.eye(128))
    put("chan_mean", (p[:, None] // 32 == p[None] // 32) / 32.0)
    put("chan_mean4", (p[:, None] // 32 == np.arange(4)[None]) / 32.0)
    put("row_mean", (p[:, None] % 32 == p[None] % 32) / 4.0)
    n, q, e = p // 64, p // 16 % 4, p % 16
    same = (n[:, None] == n[None]) & (e[:, None] == e[None])
    put("same_expert", same)
    m = np.arange(32)
    put("to_expert", (n[:, None] == m[None] // 16) & (e[:, None] == m[None] % 16))
    put("from_expert", (m[:, None] // 16 == n[None]) & (m[:, None] % 16 == e[None]))
    put("quarter", q[:, None] == np.arange(4)[None])
    put("parity", q[:, None] % 2 == np.arange(2)[None])
    put("rowsel", p[:, None] // 32 == np.arange(4)[None])
    put("colsel", p[:, None] // 8 % 4 == np.arange(4)[None])
    put("half", np.tile(np.eye(2).reshape(1, 4), (128, 1)))
    put("eps6", np.full((128, 1), 1e-6))
    put("eps5", np.full((128, 1), 1e-5))
    j = np.arange(108) % 27
    k = j % 9
    put("tapoff", np.where(j < 9, k % 3 - 1, np.where(j < 18, k // 3 - 1, 0))[:, None])
    ys = YS0 + np.arange(2 * NYP)
    xs = X0 + np.arange(XC * NXC)
    put("ytab", np.tile(-ys, (128, 1)))
    put("xtab", np.tile(-xs, (128, 1)))
    sp, xp = np.concatenate([ys[0::2], ys[1::2]]), xs[::2]
    put("yabove", np.tile(-sp - 1, (9, 1)))
    put("ybelow", np.tile(sp - 1, (9, 1)))
    put("xabove", np.tile(-xp - 2, (9, 1)))
    put("xbelow", np.tile(xp - 1, (9, 1)))
    put("taprow", np.arange(9)[:, None] // 3 == np.arange(3)[None])
    kind = np.where(p < 108, p % 27 // 9, 2)
    put("notx", np.where(kind == 0, 0.0, FAR)[:, None])
    put("noty", np.where(kind == 1, 0.0, FAR)[:, None])
    put("fromend", np.tile(XP - np.arange(XP * NXC) % XP, (128, 1)))
    put("fromstart", np.tile(np.arange(XP * NXC) % XP + 1, (128, 1)))
    put("xlow", np.tile(-(xs[::XC] + XC), (128, 1)))
    put("xhigh", np.tile(xs[::XC] - 1, (128, 1)))
    return t


def metaformer_kernel(nc, x, convw, gate_w, gate_b, w1, w2, w2b, wv, bv, wom, bom, wo, gamma, beta,
                      wct, consts, out, taps=None):
    with ExitStack() as ctx:
        def sb(name, shape, dt=F32):
            return ctx.enter_context(nc.sbuf_tensor(name, shape, dt))

        def sem(name):
            return ctx.enter_context(nc.semaphore(name))

        planes = nc.dram_tensor("planes", [NI * G * PLANE], F32, kind="Internal").ap()
        om_dram = nc.dram_tensor("om_dram", [108, NI, NY, R * HW], F32, kind="Internal").ap()
        smp_dram = nc.dram_tensor("smp_dram", [NI * G * NY, R * CG * HW], F32, kind="Internal").ap()
        short_dram = nc.dram_tensor("short_dram", [128, COLS], F32, kind="Internal").ap()

        X = sb("X", [128, COLS])
        cst = sb("cst", [128, NCONST])
        Wv_bd = sb("Wv_bd", [128, 128])
        Wo_bd = sb("Wo_bd", [128, 128])
        Wc_bd = sb("Wc_bd", [128, 128])
        Wom4 = sb("Wom4", [128, R, 108])
        vecs = sb("vecs", [128, 4])
        stats = sb("stats", [128, 4, 6])
        small = sb("small", [128, 16])
        ranges = sb("ranges", [1, 4], I32)
        words = sb("words", [1, NYP * NXC], I32)
        packed_i_sb = sb("packed_i", [NYP, NXC], I32)
        arena = sb("arena", [128, 47936])

        def area(at, n):
            return arena[:, at:at + n]

        def const(name, parts=128):
            lo, hi = CONST[name]
            return cst[0:parts, lo:hi]

        ident = const("ident")
        raw1 = area(43360, 96).rearrange("p (w c) -> p w c", w=3)
        Wom_r = area(43456, 108)
        raw = area(0, RAWN)
        Tw = area(3776, 3840)
        Sw = area(7616, 1536)
        Ew = area(9152, 512)
        Dw = area(30736, 1024)
        A = [area(10176 + i * 2376, 2376).rearrange("p (n y x) -> p n y x", n=NI, y=NY + 2) for i in range(3)]
        B = [area(26000 + i * 680, 680).rearrange("p (n y x) -> p n y x", n=NI, y=10) for i in range(3)]
        D = [area(28040 + i * 216, 216).rearrange("p (n y x) -> p n y x", n=NI, y=6) for i in range(3)]
        up = area(28688, 2048)
        XCt = area(19200, COLS)
        SQ = area(21248, COLS)
        U = area(23296, COLS)
        ln_sd = area(25400, 64)
        ln_rs = area(25464, 64)
        W1s = area(31760, 2048)[0:33, :].rearrange("p (e h) -> p e h", e=EXP)
        W2s = area(33808, 512).rearrange("p (e o) -> p e o", e=EXP)
        W2b = area(34320, 16)[0:32, :]
        gb = area(34336, 1)
        graw = area(34338, 16)
        Gw = area(34354, 256).rearrange("p (r h j) -> p r h j", r=R, h=2)
        Gh = area(34610, 64).rearrange("p (h j) -> p h j", h=2)
        LG = area(34680, 1032)
        LGr = area(35712, 1032)
        Ee = area(36744, 1024)
        E2 = area(37768, 1024)
        Pm = area(38792, 1024)
        XTs = area(39816, 2048).rearrange("p (j m) -> p j m", j=16)
        PTs = area(41864, 1024).rearrange("p (j m) -> p j m", j=8)
        FX = area(42888, 470)
        OMs = area(6912, 8192)[0:108, :].rearrange("p (n y r x) -> p n y r x", n=NI, y=NY, r=R)
        VAL = area(15104, COLS)
        T2 = area(17152, COLS)
        SMP = area(25344, COLS)
        SHT = area(27392, COLS)
        Zt = area(29440, COLS)
        dxy = area(0, 3 * TAPS)
        dx, dy, mk = (area(i * TAPS, TAPS) for i in range(3))
        hx = area(6912, XC * TAPS).rearrange("p (j t) -> p j t", j=XC)
        ay = area(29952, 2 * TAPS).rearrange("p (h t) -> p h t", h=2)
        Pt = area(34560, 2 * TAPS).rearrange("p (h t) -> p h t", h=2)
        Mt = area(39168, 2 * 2048).rearrange("p (h t) -> p h t", h=2)
        Vt = area(43264, 2 * 32 * WB).rearrange("p (h s w) -> p h s w", h=2, w=WB)
        hxs = area(6912, XC * TAPS)
        ext_half = area(34560, 4)
        ext = area(34564, 2)
        ext_g = area(34632, 16)[0:9, :].rearrange("p (i g) -> p i g", i=4)
        cmp_y = [area(34650 + i * 512, 512)[0:9, :].rearrange("p (g s) -> p g s", g=G) for i in range(2)]
        cmp_x = [area(35674 + i * 272, 272)[0:9, :].rearrange("p (g s) -> p g s", g=G) for i in range(2)]
        NACT = XP * NXC + 3
        reach = area(36220, 2 * NACT)[0:NYP, :].rearrange("p (h s) -> p h s", h=2)
        scaled = area(36360, 2 * XP * NXC)[0:NYP, :].rearrange("p (h s) -> p h s", h=2)
        first, last, word = (area(36500 + 2 * NXC * i, 2 * NXC)[0:NYP, :].rearrange("p (h s) -> p h s", h=2)
                             for i in range(3))
        kinds = area(36580, 4)[0:NYP, :].rearrange("p (i h) -> p i h", i=2)
        packed = area(36586, NXC)[0:NYP, :]
        rng_cmp = area(36740, 2 * (NXC + NYP))[0:1, :]
        packed_i = packed_i_sb[:, :]
        zeros = area(36744, ZERO)
        zero_bank = area(43264, BANK)

        psA = ctx.enter_context(nc.psum_tensor("psA", [128, COLS], F32))
        psW = ctx.enter_context(nc.psum_tensor("psW", [128, 2, BANK], F32))
        T0 = ctx.enter_context(nc.psum_tensor("T0", [128, BANK], F32))
        T1 = ctx.enter_context(nc.psum_tensor("T1", [128, BANK], F32))

        x_in, ln_cst_in, cst_in, raw_in, small_in = [sem("x_in0"), sem("x_in1")], sem("ln_cst_in"), sem("cst_in"), sem("raw_in"), sem("small_in")
        ffn_in = sem("ffn_in")
        zeroed, planes_zero = sem("zeroed"), sem("planes_zero")
        borders = sem("borders")
        w_zero, w_ready, t_ready = sem("w_zero"), sem("w_ready"), sem("t_ready")
        bd_ready = sem("bd_ready")
        ln_mean, ln_cent, ln_sq, ln_var = sem("ln_mean"), sem("ln_cent"), sem("ln_sq"), sem("ln_var")
        ln_std, ln_rstd, ln_out = sem("ln_std"), sem("ln_rstd"), sem("ln_out")
        ln_wide, ln_spread = sem("ln_wide"), sem("ln_spread")
        conv_sum, evac_act, evac_dve, conv_res = sem("conv_sum"), sem("evac_act"), sem("evac_dve"), sem("conv_res")
        up_sum, up_relu, up_mix = sem("up_sum"), sem("up_relu"), sem("up_mix")
        x_upd = sem("x_upd")
        f_gw, f_xt, f_xts, f_lg, f_lgs = sem("f_gw"), sem("f_xt"), sem("f_xts"), sem("f_lg"), sem("f_lgs")
        f_top, f_ex, f_cand, f_ct, f_pack = sem("f_top"), sem("f_ex"), sem("f_cand"), sem("f_ct"), sem("f_pack")
        f_back, f_msk, f_max, f_rest = sem("f_back"), sem("f_msk"), sem("f_max"), sem("f_rest")
        f_exp, f_exp2, f_den, f_rden, f_dif, f_p = (sem("f_exp"), sem("f_exp2"), sem("f_den"), sem("f_rden"),
                                                    sem("f_dif"), sem("f_p"))
        f_pt, f_pts, f_pool, f_pooled = sem("f_pt"), sem("f_pts"), sem("f_pool"), sem("f_pooled")
        f_h, f_gelu, f_o, f_ob, f_ot, f_obs, f_y = (sem("f_h"), sem("f_gelu"), sem("f_o"), sem("f_ob"),
                                                    sem("f_ot"), sem("f_obs"), sem("f_y"))
        f_one = sem("f_one")
        d_val, d_vals, d_vst, d_om, d_oma, d_omv, d_omst, d_dxy = (
            sem("d_val"), sem("d_vals"), sem("d_vst"), sem("d_om"), sem("d_oma"), sem("d_omv"), sem("d_omst"),
            sem("d_dxy"))
        d_short, d_ext, d_all, d_rng, d_cmp = sem("d_short"), sem("d_ext"), sem("d_all"), sem("d_rng"), sem("d_cmp")
        d_kext, d_tr, d_reach, d_act, d_words, words_in = (sem("d_kext"), sem("d_tr"), sem("d_reach"), sem("d_act"),
                                                           sem("d_words"), sem("words_in"))
        hat_abs, hx_ready, hx_free, ay_ready, ay_free = (
            sem("hat_abs"), sem("hx_ready"), sem("hx_free"), sem("ay_ready"), sem("ay_free"))
        ay_masked = sem("ay_masked")
        v_loaded, v_free = [sem("v_loaded0"), sem("v_loaded1")], [sem("v_free0"), sem("v_free1")]
        p_mult, p_part, p_ready, w_sum, m_ready, acc_sum = (
            sem("p_mult"), sem("p_part"), sem("p_ready"), sem("w_sum"), sem("m_ready"), sem("acc_sum"))
        p_half, hat_dve = sem("p_half"), sem("hat_dve")
        v_zero, d_acc = sem("v_zero"), sem("d_acc")
        z_bank, acc_zero = sem("z_bank"), sem("acc_zero")
        d_smp, d_smst, d_smld, d_shld, d_wo, d_st, d_agg, d_mean, d_dev, d_varm = (
            sem("d_smp"), [sem("d_smst0"), sem("d_smst1")], [sem("d_smld0"), sem("d_smld1")], sem("d_shld"), sem("d_wo"), sem("d_st"), sem("d_agg"),
            sem("d_mean"), sem("d_dev"), sem("d_varm"))
        d_std, d_sc, d_bn, d_zs, d_wc = sem("d_std"), sem("d_sc"), sem("d_bn"), sem("d_zs"), sem("d_wc")
        stored = sem("stored")

        def bank(t, q):
            return t[:, q * BANK:(q + 1) * BANK]

        def inner(t, n, y0, ny, step=1, dx=0, w=None, r0=0, r1=128):
            w = w or t.shape[3] - 2
            nn = slice(0, NI) if n is None else slice(n, n + 1)
            return t[r0:r1, nn, y0:y0 + (ny - 1) * step + 1:step, dx:dx + (w - 1) * step + 1:step]

        CONVS = [("e0b0c1", A[0], A[1], None, None, 64), ("e0b0c2", A[1], A[2], A[0], None, 64),
                 ("e0b1c1", A[2], A[1], None, None, 64), ("e0b1c2", A[1], A[0], A[2], None, 64),
                 ("e1b0c1", A[0], B[0], None, None, 32), ("e1b0c2", B[0], B[1], None, A[0], 32),
                 ("e1b1c1", B[1], B[0], None, None, 32), ("e1b1c2", B[0], B[2], B[1], None, 32),
                 ("e2b0c1", B[2], D[0], None, None, 16), ("e2b0c2", D[0], D[1], None, B[2], 16),
                 ("e2b1c1", D[1], D[0], None, None, 16), ("e2b1c2", D[0], D[2], D[1], None, 16)]
        CHUNKS = []
        counts = {"act": 0, "dve": 0}
        FIRST_CHUNK = []
        for i, cv in enumerate(CONVS):
            FIRST_CHUNK.append(len(CHUNKS))
            for q in range(NQ if cv[5] == 64 else 1):
                who = "dve" if cv[3] is not None else "act"
                counts[who] += 1
                CHUNKS.append((i, q, who, counts[who]))

        def chunk_out(eng, j):
            _, _, who, n = CHUNKS[j]
            eng.wait_ge(evac_act if who == "act" else evac_dve, n)

        def source_chunks(i, q):
            if i == 0:
                return None
            n = FIRST_CHUNK[i] - FIRST_CHUNK[i - 1]
            return FIRST_CHUNK[i - 1] + ((1 if q < 2 else 3) if n == NQ and CONVS[i][5] == 64 else n - 1)

        def chunk_view(size, q):
            return (q // 2, q % 2 * 8, 8) if size == 64 else (None, 0, size // R)

        def psum_view(j, size):
            n, y0, ny = chunk_view(size, CHUNKS[j][1])
            cols = (1 if n is not None else NI) * ny * size
            return bank(psA, j % NQ)[:, 0:cols].rearrange(
                "p (n y x) -> p n y x", n=1 if n is not None else NI, y=ny)

        T3 = Tw.rearrange("p (v k m) -> p v k m", v=len(S1), k=3)
        S3 = Sw.rearrange("p (v b k m) -> p v b k m", v=2, b=2, k=3)
        E3 = Ew.rearrange("p (v b m) -> p v b m", v=2, b=2)
        D3 = Dw.rearrange("p (v h l m) -> p v h l m", v=2, h=2, l=2)
        raw3 = raw[:, 0:RAW3].rearrange("p (v k e o) -> p v k e o", v=12, k=3, e=3)
        raw_ds = raw[:, RAW3:RAW3 + 64].rearrange("p (v o) -> p v o", v=2)
        raw_up = raw[:, RAW3 + 64:RAWN].rearrange("p (v l m) -> p v l m", v=2, l=2)

        block = ctx.enter_context(nc.Block())


        OM_ACT = 12
        OM_OUT = [("act" if k % 2 == 0 or k >= 8 else "dve", k // 2 + 1 if k < 8 else k - 3) for k in range(R * NQ)]

        def om_bank(k):
            return [psW[:, 0], psW[:, 1], T0, T1][k % 4][0:108, :].rearrange("p (y x) -> p y x", x=HW)

        def om_rows(k):
            q, r = divmod(k, R)
            return OMs[:, q // 2, q % 2 * 8:q % 2 * 8 + 8, r, :]

        def dcn_load_tiles(sp, l):
            for n in range(NI):
                for half in range(2):
                    q = 2 * n + half
                    sp.wait_ge(d_oma, OM_ACT * l + (2, 4, 8, 12)[q])
                    if n == 0:
                        sp.wait_ge(d_omv, 4 * l + 2 * q + 2)
                    y = slice(8 * half, 8 * half + 8)
                    sp.dma_start(om_dram[:, n, y], OMs[:, n, y].rearrange("p y r x -> p y (r x)"))\
                        .then_inc(d_omst, 16)
                sp.wait_ge(d_omst, 64 * l + 32 * (n + 1))
                if l == 0 and n == 0:
                    sp.wait_ge(f_y, NQ)
                for g in range(G):
                    ng = n * G + g
                    src = om_dram[g * 27:(g + 1) * 27, n].rearrange("j y t -> y j t")
                    sp.dma_start(dxy[16 * ng:16 * ng + 16, :].rearrange("p (j t) -> p j t", j=27), src)\
                        .then_inc(d_dxy, 16)

            sp.wait_ge(d_vals, NQ * (l + 1))
            if l == 0:
                sp.wait_ge(planes_zero, 16)
            for n in range(NI):
                for g in range(G):
                    at = (n * G + g) * PLANE - YS0 * CG * PCOLS - X0
                    dst = bass.AP(planes.tensor, at, [[PCOLS, 32], [R * CG * PCOLS, NY], [1, HW]])
                    sp.dma_start(dst, VAL[32 * g:32 * g + 32, n * 1024:(n + 1) * 1024].rearrange(
                        "p (y x) -> p y x", x=HW)).then_inc(d_vst, 16)

        def load_ffn(sp, f):
            if f == 1:
                sp.wait_ge(d_smp, 2 * NQ)
            sp.dma_start(W1s, w1[f].rearrange("e d h -> d e h")).then_inc(ffn_in, 16)
            sp.dma_start(W2s, w2[f, :, 0:HID].rearrange("e h o -> h e o")).then_inc(ffn_in, 16)
            sp.dma_start(W2b, w2b[f]).then_inc(ffn_in, 16)
            sp.dma_start(gb, bass.AP(gate_b.tensor, f * EXP, [[0, 8], [1, EXP], [1, 1]])).then_inc(ffn_in, 16)
            for r in range(R):
                sp.dma_start(graw[32 * r:32 * r + 32, :], gate_w[f]).then_inc(ffn_in, 16)

        FFN_IN = 16 * (4 + R)

        def walk(eng, pairs, chunks, body, start=None, first=None, chunk_end=None,
                 ends=None):
            xlo = eng.value_load(ranges[0:1, 0:1], min_val=0, max_val=NXC - 1)
            xhi = eng.value_load(ranges[0:1, 1:2], min_val=1, max_val=NXC)
            ylo = eng.value_load(ranges[0:1, 2:3], min_val=0, max_val=NYP - 1)
            yhi = eng.value_load(ranges[0:1, 3:4], min_val=1, max_val=NYP)
            with eng.Fori(xlo, xhi) as cx:
                nch = eng.snap(chunks)
                if start is not None:
                    start(cx, ylo, nch)
                if first is not None:
                    first(cx, ylo, nch, eng.snap(pairs))
                    eng.reg_add(pairs, pairs, 1)
                def others(iy0):
                    with eng.Fori(iy0, yhi) as iy:
                        if ends is not None:
                            ends(cx + 1, xhi, iy, ylo, yhi)
                        body(cx, iy, nch, eng.snap(pairs))
                        eng.reg_add(pairs, pairs, 1)

                if first is None:
                    others(ylo)
                else:
                    with eng.If(ylo + 1 < yhi):
                        others(ylo + 1)
                        eng.nop()
                if chunk_end is not None:
                    chunk_end()
                eng.reg_add(chunks, chunks, 1)
            return eng.snap(pairs)

        def load_word(eng, word_reg, cx, iy):
            eng.reg_load(word_reg, words[0:1, bass.ds(iy * NXC + cx, 1)])
            return eng.snap(word_reg)

        def hold(eng, value, lo, hi):
            reg = eng.alloc_register(f"held{next(held)}")
            eng.reg_mov(reg, value)
            return eng.snap(reg, min_val=lo, max_val=hi)

        held = itertools.count()

        def row_fields(eng, w, h):
            b = 8 * h
            return (hold(eng, (w >> b) & 7, 0, XP - 1), hold(eng, (w >> (b + 3)) & 7, 1, XP),
                    hold(eng, (w >> (b + 6)) & 1, 0, 1), hold(eng, ((w >> (b + 7)) & 1) * TRI, 0, TRI))

        def fold_taps(i, taps, fold):
            a, b = (Pt[:, i, o * 256:(o + fold) * 256] for o in (taps - 2 * fold, taps - fold))
            return a, a, b, ALU.add

        def by_kind(eng, full, run):
            with eng.If(full > 0):
                run(TAPS_FULL)
                eng.nop()
            with eng.If(full < 1):
                run(TAPS_TWO)
                eng.nop()

        def counters(eng, names=("pairs_run", "chunks_run")):
            regs = []
            for name in names:
                reg = eng.alloc_register(name)
                eng.reg_mov(reg, 0)
                regs.append(reg)
            return regs

        @block.sync
        def _(sp):
            sp.dma_start(cst[:, 0:FIRST_CONST], consts[:, 0:FIRST_CONST]).then_inc(ln_cst_in, 16)
            for n in range(NI):
                for r in range(R):
                    src = bass.AP(x.tensor, n * C * HW * HW + r * HW, [[HW * HW, C], [R * HW, NY], [1, HW]])
                    sp.dma_start(X[32 * r:32 * r + 32, n * 1024:(n + 1) * 1024].rearrange(
                        "p (y x) -> p y x", x=HW), src).then_inc(x_in[n], 16)
            sp.dma_start(cst[:, FIRST_CONST:], consts[:, FIRST_CONST:]).then_inc(cst_in, 16)
            for r in range(R):
                rows = slice(32 * r, 32 * r + 32)
                sp.dma_start(raw1[rows, 0, :], wv).then_inc(small_in, 16)
                sp.dma_start(raw1[rows, 1, :], bass.AP(wo.tensor, r * CG * C, [[0, 4], [C, CG], [1, C]]))\
                    .then_inc(small_in, 16)
                sp.dma_start(raw1[rows, 2, :], wct).then_inc(small_in, 16)
                sp.dma_start(Wom_r[rows, :], wom).then_inc(small_in, 16)
            for g in range(G):
                sp.dma_start(vecs[32 * g:32 * g + 32, 0:1], bass.AP(bv.tensor, g * CG, [[0, R], [1, CG], [1, 1]]))\
                    .then_inc(small_in, 16)
            sp.dma_start(vecs[:, 1:2], bass.AP(gamma.tensor, 0, [[0, R], [1, C], [1, 1]])).then_inc(small_in, 16)
            sp.dma_start(vecs[:, 2:3], bass.AP(beta.tensor, 0, [[0, R], [1, C], [1, 1]])).then_inc(small_in, 16)
            sp.dma_start(vecs[0:108, 3:4], bass.AP(bom.tensor, 0, [[1, 108], [1, 1]])).then_inc(small_in, 16)
            load_ffn(sp, 0)

            pairs, chunks = counters(sp)
            for l in range(2):
                if l == 0:
                    sp.wait_ge(ln_out, 3 * NQ)
                    sp.dma_start(short_dram, U).then_inc(d_short, 16)
                dcn_load_tiles(sp, l)
                sp.wait_ge(d_words, l + 1)
                sp.dma_start(words[:, :], packed_i).then_inc(words_in, 16)

                def load_bands(cx, iy, nch, done):
                    sp.wait_ge(d_vst, 128 * (l + 1))
                    sp.wait_ge(acc_zero, NQ * (l + 1))
                    for h in range(2):
                        sp.wait_ge(v_free[h], done + 1)
                        for ng in range(NI * G):
                            src = bass.AP(planes.tensor, (iy * 2 + h) * (CG * PCOLS) + cx * XC + ng * PLANE,
                                          [[R * CG * PCOLS, NY], [PCOLS, R * CG], [1, WB]])
                            sp.dma_start(Vt[16 * ng:16 * ng + 16, h], src).then_inc(v_loaded[h], 16)

                walk(sp, pairs, chunks, load_bands)
                sp.wait_ge(d_smp, NQ * (l + 1))
                for n in range(NI):
                    half = slice(64 * n, 64 * n + 64)
                    sp.dma_start(smp_dram[half], SMP[half]).then_inc(d_smst[n], 16)
                for ng in range(NI * G):
                    n, g = divmod(ng, G)
                    if g == 0:
                        sp.wait_ge(d_smst[n], 16 * (l + 1))
                    src = bass.AP(smp_dram.tensor, ng * NY * 2048, [[HW, 32], [2048, NY], [1, HW]])
                    sp.dma_start(VAL[32 * g:32 * g + 32, n * 1024:(n + 1) * 1024].rearrange(
                        "p (y x) -> p y x", x=HW), src).then_inc(d_smld[n], 16)
                if l == 1:
                    sp.dma_start(SHT, short_dram).then_inc(d_shld, 16)
            load_ffn(sp, 1)
            for q in range(NQ):
                sp.wait_ge(x_upd, 3 * NQ + q + 1)
                n, half = divmod(q, 2)
                for r in range(R):
                    dst = bass.AP(out.tensor, n * C * HW * HW + half * 8 * R * HW + r * HW,
                                  [[HW * HW, C], [R * HW, 8], [1, HW]])
                    sp.dma_start(dst, bank(X, q)[32 * r:32 * r + 32, :].rearrange("p (y x) -> p y x", x=HW))\
                        .then_inc(stored, 16)
            sp.wait_ge(stored, 16 * R * NQ)

        @block.gpsimd
        def _(pool):
            for r in range(R):
                pool.dma_start(raw[32 * r:32 * r + 32, :], convw).then_inc(raw_in, 16)
            pool.memset(Tw, 0.0).then_inc(w_zero, 1)
            pool.memset(area(7616, 2048), 0.0).then_inc(w_zero, 1)
            pool.memset(Dw, 0.0).then_inc(w_zero, 1)
            pool.wait_ge(w_zero, 3)
            pool.wait_ge(raw_in, 16 * R)
            made = [0]

            def copy(dst, src):
                if made[0]:
                    pool.wait_ge(w_ready, made[0])
                pool.tensor_copy(dst, src).then_inc(w_ready, 1)
                made[0] += 1

            for ro in range(R):
                for ky in range(3):
                    b, ri = divmod(2 * ro + ky - 1, R)
                    if b >= 0:
                        for v in range(2):
                            copy(S3[32 * ri:32 * ri + 32, v, b, :, 32 * ro:32 * ro + 32],
                                             raw3[32 * ri:32 * ri + 32, len(S1) + v, :, 2 - ky, :])
                b, ri = divmod(2 * ro, R)
                copy(E3[32 * ri:32 * ri + 32, :, b, 32 * ro:32 * ro + 32],
                                 raw_ds[32 * ri:32 * ri + 32, :, :])
            for ri in range(R):
                for v in range(2):
                    copy(D3[32 * ri:32 * ri + 32, v, ri // 2, :, (ri % 2) * 64:(ri % 2) * 64 + 64],
                                     raw_up[32 * ri:32 * ri + 32, v])
            pool.wait_ge(w_ready, made[0])
            pool.memset(zeros, 0.0).then_inc(zeroed, 1)
            pool.wait_ge(zeroed, 1)
            pool.dma_start(planes.rearrange("(p a w) -> p a w", p=128, a=4),
                           zeros.rearrange("p (a w) -> p a w", a=1).broadcast_to([128, 4, ZERO]))\
                .then_inc(planes_zero, 16)
            pairs, chunks, shifts, word_reg, masked, third, skip, limit, halves = counters(
                pool, ("pairs_run", "chunks_run", "shifts_run", "word", "masked", "third", "skip", "limit", "halves"))
            pool.reg_mov(masked, 1)

            def mask_third(h, rows, t):
                n, m = pool.snap(shifts), pool.snap(masked)
                pool.wait_ge(p_ready, n + LEAD)
                pool.wait_ge(ay_ready, rows)
                pool.wait_ge(ay_masked, m)
                pool.reg_add(masked, masked, 1)
                a, m = (x[:, bass.ds(t * TRI, TRI)] for x in (ay[:, h, :], mk))
                pool.tensor_tensor(a, a, m, ALU.mult).then_inc(ay_masked, 1)
            for l in range(2):
                pool.wait_ge(d_ext, 2 * (l + 1))
                pool.partition_all_reduce(small[:, 4:8], small[:, 0:4], 128, bass.bass_isa.ReduceOp.max)\
                    .then_inc(d_all, 1)
                pool.wait_ge(d_all, l + 1)
                pool.wait_ge(d_rng, l + 1)
                pool.wait_ge(words_in, 16 * (l + 1))
                pool.wait_ge(d_dxy, 128 * (l + 1))
                pool.sem_inc(p_ready, LEAD)
                if l > 0:
                    pool.reg_add(shifts, shifts, LEAD)
                for t in range(3):
                    mask_third(0, pool.snap(pairs) * 2 + 1, t)

                def find_ends(next_cx, xhi, iy, ylo, yhi):
                    pool.reg_mov(limit, 0)
                    with pool.If(iy > ylo):
                        pool.reg_mov(limit, 3)
                    pool.reg_mov(skip, 0)
                    with pool.If(iy + 1 >= yhi):
                        with pool.If(next_cx >= xhi):
                            pool.reg_mov(skip, 3)
                        pool.nop()

                def folds(cx, iy, nch, done):
                    w = load_word(pool, word_reg, cx, iy)
                    for h in range(2):
                        lo, hi, full, off = row_fields(pool, w, h)
                        pool.reg_mov(third, 0 if h == 0 else pool.snap(skip))
                        next_row = done * 2 + (h + 2)

                        def run(kind):
                            taps, part, steps = kind
                            with pool.Fori(lo, hi):
                                n, m = pool.snap(shifts), pool.snap(masked)
                                for i in range(2):
                                    pool.wait_ge(p_part, n + (LEAD + i + 1))
                                    pool.wait_ge(p_ready, n + (LEAD + i))
                                    if i == 0:
                                        pool.wait_ge(ay_masked, m)
                                    left = taps - part
                                    for step in steps:
                                        if step != steps[0]:
                                            pool.wait_ge(p_half, pool.snap(halves) + 1)
                                            pool.reg_add(halves, halves, 1)
                                        ins = pool.tensor_tensor(*fold_taps(i, left, step))
                                        left -= step
                                        ins.then_inc(p_ready if step == steps[-1] else p_half, 1)
                                pool.reg_add(shifts, shifts, 2)
                                with pool.If(pool.snap(third) < pool.snap(limit)):
                                    mask_third(1 - h, next_row, hold(pool, third, 0, 2))
                                    pool.reg_add(third, third, 1)

                        by_kind(pool, full, run)
                        with pool.If(pool.snap(third) < 3):
                            with pool.Fori(hold(pool, third, 0, 2), 3) as t:
                                mask_third(1 - h, next_row, t)
                            pool.nop()

                walk(pool, pairs, chunks, folds, ends=find_ends)
            pool.wait_ge(planes_zero, 16)

        W_ALL = 22 + 4 + 2 * R

        def banded_act(act):
            act.wait_ge(w_zero, 1)
            act.wait_ge(raw_in, 16 * R)
            for r in (0, 3):
                lo, hi = max(r - 1, 0), min(r + 2, R)
                src = raw3[32 * r:32 * r + 32, 0:len(S1), :, lo - r + 1:hi - r + 1, :]
                act.activation(T3[32 * r:32 * r + 32, :, :, 32 * lo:32 * hi].rearrange("p v k m -> p (v k) m"),
                               src.rearrange("p v k e o -> p (v k) (e o)"), ACT.Copy).then_inc(t_ready, 1)

        def banded_dve(dve):
            dve.wait_ge(w_zero, 1)
            dve.wait_ge(raw_in, 16 * R)
            for r in (1, 2):
                src = raw3[32 * r:32 * r + 32, 0:len(S1), :, 0:3, :]
                dve.tensor_copy(T3[32 * r:32 * r + 32, :, :, 32 * r - 32:32 * r + 64].rearrange(
                    "p v k m -> p (v k) m"), src.rearrange("p v k e o -> p (v k) (e o)")).then_inc(t_ready, 1)

        def ln_bank(q):
            return [psW[:, 0], psW[:, 1], T0, T1][q]

        def ln_pe(pe, i, src, ready):
            for q in range(NQ):
                ready(pe, q)
                pe.matmul(bank(psA, q), const("chan_mean"), bank(src, q), start=True, stop=True)\
                    .then_inc(ln_mean, 1)
            for q in range(NQ):
                pe.wait_ge(ln_sq, NQ * i + q + 1)
                for m in range(4 * q, 4 * q + 4):
                    mm = pe.matmul(ln_bank(q)[:, 4 * (m % 4):4 * (m % 4) + 4], SQ[:, 128 * m:128 * m + 128], const("chan_mean4"),
                                   start=True, stop=True, skip_group_check=True)
                mm.then_inc(ln_var, 1)
            for q in range(NQ):
                pe.wait_ge(ln_spread, NQ * i + q + 1)
                for m in range(4 * q, 4 * q + 4):
                    mm = pe.matmul(psA[:, 128 * m:128 * m + 128],
                                   SQ[:, 128 * m:128 * m + 128], ident, start=True, stop=True, skip_group_check=True)
                mm.then_inc(ln_wide, 1)

        def ln_act(act, i, eps):
            for q in range(NQ):
                act.wait_ge(ln_cent, NQ * i + q + 1)
                act.activation(bank(SQ, q), bank(XCt, q), ACT.Square).then_inc(ln_sq, 1)
            for q in range(NQ):
                act.wait_ge(ln_var, NQ * i + q + 1)
                act.activation(ln_sd[:, 16 * q:16 * q + 16], ln_bank(q)[:, 0:16], ACT.Sqrt, bias=const(eps))\
                    .then_inc(ln_std, 1)

        def ln_dve(dve, i, src, ready, dst):
            for q in range(NQ):
                ready(dve, q)
                dve.wait_ge(ln_mean, NQ * i + q + 1)
                dve.tensor_tensor(bank(XCt, q), bank(src, q), bank(psA, q), ALU.subtract).then_inc(ln_cent, 1)
            for q in range(NQ):
                dve.wait_ge(ln_std, NQ * i + q + 1)
                dve.reciprocal(ln_rs[:, 16 * q:16 * q + 16], ln_sd[:, 16 * q:16 * q + 16]).then_inc(ln_rstd, 1)
                dve.wait_ge(ln_rstd, NQ * i + q + 1)
                dve.tensor_copy(bank(SQ, q).rearrange("p (m c) -> p m c", c=C),
                                ln_rs[:, 16 * q:16 * q + 16].rearrange("p (m c) -> p m c", c=1).broadcast_to(
                                    [128, 16, C])).then_inc(ln_spread, 1)
            for q in range(NQ):
                dve.wait_ge(ln_wide, NQ * i + q + 1)
                o, a, b = dst(q), bank(XCt, q), bank(psA, q)
                if len(o.shape) == 3:
                    a, b = (t.rearrange("p (y x) -> p y x", x=HW) for t in (a, b))
                dve.tensor_tensor(o, a, b, ALU.mult).then_inc(ln_out, 1)

        def x_loaded(eng, q):
            if q % 2 == 0:
                eng.wait_ge(x_in[q // 2], 16 * R)

        def x_updated(stage):
            return lambda eng, q: eng.wait_ge(x_upd, NQ * stage + q + 1)

        def unet_pe(pe):
            pe.wait_ge(t_ready, R)
            pe.wait_ge(raw_in, 16 * R)
            pe.wait_ge(borders, 18)
            for j, (i, q, _, _) in enumerate(CHUNKS):
                name, src, _, _, ds_src, size = CONVS[i]
                if i == 0:
                    pe.wait_ge(ln_out, 2 if q < 2 else 4)
                else:
                    chunk_out(pe, source_chunks(i, q))
                if j >= NQ:
                    chunk_out(pe, j - NQ)
                n, y0, ny = chunk_view(size, q)
                ps = psum_view(j, size)
                if name in S1:
                    v, first = S1.index(name), True
                    for k in range(3):
                        pe.matmul(ps, T3[:, v, k, :], inner(src, n, y0 + 1, ny, 1, k), start=first, stop=False,
                                  skip_group_check=True)
                        first = False
                    for k in range(3):
                        pe.matmul(ps[0:32], raw3[96:128, v, k, 2, :], inner(src, n, y0, ny, 1, k, r0=96),
                                  start=False, stop=False, skip_group_check=True, tile_position=(96, 0))
                        mm = pe.matmul(ps[96:128], raw3[0:32, v, k, 0, :],
                                       inner(src, n, y0 + 2, ny, 1, k, r1=32), start=False, stop=True,
                                       skip_group_check=True, tile_position=(0, 96))
                    if ds_src is not None:
                        pe.wait_ge(w_ready, W_ALL)
                        u = 0 if size == 32 else 1
                        for b in range(2):
                            mm = pe.matmul(ps, E3[:, u, b, :], inner(ds_src, n, 1 + b, ny, 2, 1, size),
                                           start=False, stop=True, skip_group_check=True)
                else:
                    pe.wait_ge(w_ready, W_ALL)
                    v = S2.index(name)
                    for b in range(2):
                        for k in range(3):
                            pe.matmul(ps, S3[:, v, b, k, :], inner(src, n, 1 + b, ny, 2, k, size),
                                      start=b == 0 and k == 0, stop=False, skip_group_check=True)
                    for k in range(3):
                        mm = pe.matmul(ps[0:32], raw3[96:128, len(S1) + v, k, 2, :],
                                       inner(src, n, 0, ny, 2, k, size, r0=96), start=False, stop=True,
                                       skip_group_check=True, tile_position=(96, 0))
                mm.then_inc(conv_sum, 1)
            chunk_out(pe, len(CHUNKS) - 1)
            for h in range(2):
                for l in range(2):
                    o = bank(psA, 0).rearrange("p (n y a x b) -> p n y a x b", n=NI, y=4, a=2, b=2)[:, :, :, h, :, l]
                    for n in range(NI):
                        mm = pe.matmul(o[:, n], D3[:, 0, h, l, :], inner(D[2], n, 1, 4, 1, 1)[:, 0],
                                       start=True, stop=True, skip_group_check=True)
            mm.then_inc(up_sum, 1)
            pe.wait_ge(up_mix, 1)
            for q in range(NQ):
                n, half = divmod(q, 2)
                for h in range(2):
                    for l in range(2):
                        o = bank(psA, q).rearrange("p (y a x b) -> p y a x b", y=4, a=2, b=2)[:, :, h, :, l]
                        mm = pe.matmul(o, D3[:, 1, h, l, :], inner(B[0], n, 1 + 4 * half, 4, 1, 1)[:, 0],
                                       start=True, stop=True, skip_group_check=True)
                mm.then_inc(up_sum, 1)

        def unet_act(act):
            for j, (i, q, who, _) in enumerate(CHUNKS):
                if who != "act":
                    continue
                _, _, dst, _, _, size = CONVS[i]
                n, y0, ny = chunk_view(size, q)
                act.wait_ge(conv_sum, j + 1)
                act.activation(inner(dst, n, y0 + 1, ny, 1, 1), psum_view(j, size), ACT.Relu, scale=BN_S)\
                    .then_inc(evac_act, 1)
            act.wait_ge(up_sum, 1)
            act.activation(bank(up, 0), bank(psA, 0), ACT.Relu, scale=BN_S * BN_S).then_inc(up_relu, 1)
            for q in range(NQ):
                act.wait_ge(up_sum, q + 2)
                if q == 0:
                    act.wait_ge(up_mix, 1)
                act.activation(bank(up, q), bank(psA, q), ACT.Relu, scale=BN_S * BN_S).then_inc(up_relu, 1)

        def unet_dve(dve):
            done = 0
            for j, (i, q, who, _) in enumerate(CHUNKS):
                if who != "dve":
                    continue
                _, _, dst, res, _, size = CONVS[i]
                n, y0, ny = chunk_view(size, q)
                o, rr, ps = inner(dst, n, y0 + 1, ny, 1, 1), inner(res, n, y0 + 1, ny, 1, 1), psum_view(j, size)
                dve.wait_ge(conv_sum, j + 1)
                if i == 1:
                    dve.wait_ge(ln_out, NQ)
                if done:
                    dve.wait_ge(evac_dve, done)
                if size < 64:
                    chunk_out(dve, FIRST_CHUNK[i] - 2)
                for m in range(o.shape[1]):
                    ins = dve.scalar_tensor_tensor(out=o[:, m], in0=ps[:, m], scalar=BN_S, in1=rr[:, m],
                                                   op0=ALU.mult, op1=ALU.add)
                ins.then_inc(conv_res, 1)
                done += 1
                dve.wait_ge(conv_res, done)
                dve.tensor_scalar(o, o, 0.0, None, ALU.max).then_inc(evac_dve, 1)
            dve.wait_ge(evac_dve, done)
            dve.wait_ge(up_relu, 1)
            for n in range(NI):
                o = inner(B[0], n, 1, 8, 1, 1)[:, 0]
                ins = dve.scalar_tensor_tensor(
                    out=o, in0=inner(B[2], n, 1, 8, 1, 1)[:, 0], scalar=BN_S,
                    in1=bank(up, 0)[:, n * 256:(n + 1) * 256].rearrange("p (y x) -> p y x", x=32),
                    op0=ALU.mult, op1=ALU.add)
            ins.then_inc(up_mix, 1)
            for q in range(NQ):
                n, half = divmod(q, 2)
                u3 = bank(up, q).rearrange("p (y x) -> p y x", x=HW)
                dve.wait_ge(up_relu, q + 2)
                dve.scalar_tensor_tensor(out=u3, in0=inner(A[0], n, 1 + 8 * half, 8, 1, 1)[:, 0], scalar=BN_S,
                                         in1=u3, op0=ALU.mult, op1=ALU.add).then_inc(up_mix, 1)
                dve.wait_ge(up_mix, q + 2)
                dve.tensor_tensor(bank(X, q), bank(X, q), bank(up, q), ALU.add).then_inc(x_upd, 1)

        top8 = FX[:, 0:8]
        spread = FX[:, 8:40]
        cand = FX[0:32, 40:72]
        best = FX[0:32, 72:80]
        cand_rest = FX[0:32, 80:112]
        pack = FX[0:32, 112:145]
        picked = FX[:, 145:177]
        keep = FX[:, 177:185]
        drop = FX[:, 185:193]
        nmax = FX[:, 193:194]
        chosen = FX[:, 194:202]
        esum = FX[:, 202:203]
        rden = FX[:, 203:204]
        pooled = FX[0:33, 204:236]
        hid = FX[:, 236:268]
        oexp = FX[0:32, 268:396]
        OB = FX[:, 396:460].rearrange("p (h o) -> p h o", h=2)

        def ffn_pe(pe, f):
            for j in range(16):
                pe.wait_ge(ln_out, NQ * (1 if f == 0 else 3) + j // 4 + 1)
                mm = pe.transpose(psA[:, 128 * j:128 * j + 128], U[:, 128 * j:128 * j + 128], ident)
                if j % 4 == 3:
                    mm.then_inc(f_xt, 1)
            pe.wait_ge(f_gw, 2 * f + 2)
            for b in range(2):
                for pr in range(4):
                    for r in range(R):
                        for h in range(2):
                            n, quarter = pr // 2, 2 * (pr % 2) + h
                            o = psW[32 * pr:32 * pr + 32, b, :].rearrange("p (y r x) -> p y r x", y=2, r=R)[:, :, r]
                            at = n * 1024 + (quarter * 4 + 2 * b) * HW
                            mm = pe.matmul(o, Gw[:, r, h, :],
                                           U[:, at:at + 128].rearrange("p (y x) -> p y x", x=HW),
                                           start=r == 0 and h == 0, stop=r == 3 and h == 1,
                                           skip_group_check=True, tile_position=(0, 32 * pr))
                mm.then_inc(f_lg, 1)
            pe.wait_ge(f_ex, f + 1)
            pe.matmul(T0[0:32, 0:32], const("to_expert"), spread, start=True, stop=True).then_inc(f_cand, 1)
            pe.wait_ge(f_pack, 2 * f + 2)
            pe.matmul(T1[:, 0:33], const("from_expert", 32), pack, start=True, stop=True).then_inc(f_back, 1)
            pe.wait_ge(f_exp, f + 1)
            pe.matmul(T0[:, 0:1], const("same_expert"), esum, start=True, stop=True).then_inc(f_den, 1)
            for j in range(8):
                pe.wait_ge(f_p, 2 * f + j // 4 + 1)
                mm = pe.transpose(psW[:, j // 4, 128 * (j % 4):128 * (j % 4) + 128], Pm[:, 128 * j:128 * j + 128],
                                  ident)
                if j % 4 == 3:
                    mm.then_inc(f_pt, 1)
            pe.wait_ge(f_xts, NQ * (f + 1))
            pe.wait_ge(f_pts, 2 * (f + 1))
            for n in range(NI):
                for quarter in range(4):
                    for b in range(2):
                        for r in range(R):
                            at = n * 64 + quarter * 16
                            mm = pe.matmul(T1[0:32, n * 16:n * 16 + 16],
                                           XTs[:, n * 8 + quarter * 2 + b, 32 * r:32 * r + 32],
                                           PTs[:, 4 * b + r, at:at + 16],
                                           start=n == quarter == b == r == 0, stop=quarter == 3 and b == 1 and r == 3,
                                           skip_group_check=True)
            mm.then_inc(f_pool, 1)
            pe.wait_ge(f_pooled, f + 1)
            for e in range(EXP):
                mm = pe.matmul(T0[:, 2 * e:2 * e + 2], W1s[:, e, :], pooled[:, e:e + 17:16], start=True, stop=True,
                               skip_group_check=True)
            mm.then_inc(f_h, 1)
            pe.wait_ge(f_gelu, f + 1)
            for e in range(EXP):
                mm = pe.matmul(T1[0:32, 2 * e:2 * e + 2], W2s[:, e, :], hid[:, 2 * e:2 * e + 2], start=True,
                               stop=True, skip_group_check=True)
            mm.then_inc(f_o, 1)
            pe.wait_ge(f_ob, f + 1)
            pe.transpose(T0[:, 0:32], oexp, ident[0:32, 0:32]).then_inc(f_ot, 1)
            pe.wait_ge(f_obs, f + 1)
            for q in range(NQ):
                for h in range(2):
                    for r in range(R):
                        o = psA[32 * r:32 * r + 32, q * BANK + h * 256:q * BANK + h * 256 + 256]
                        mm = pe.matmul(o.rearrange("p (b t) -> p b t", b=2), OB[32 * q:32 * q + 32, h, :],
                                       Pm[32 * q:32 * q + 32, :].rearrange("p (b r t) -> p b r t", b=2, r=R)[:, :, r],
                                       start=True, stop=True, skip_group_check=True,
                                       tile_position=(32 * q, 32 * r))
                mm.then_inc(f_y, 1)

        def ffn_act(act, f):
            if f == 0:
                act.wait_ge(planes_zero, 16)
            for q in range(NQ):
                act.wait_ge(f_xt, NQ * f + q + 1)
                act.activation(XTs[:, 4 * q:4 * q + 4, :].rearrange("p j m -> p (j m)"), bank(psA, q), ACT.Copy)\
                    .then_inc(f_xts, 1)
            act.wait_ge(f_max, f + 1)
            act.activation(Ee, LG[:, 0:TOK], ACT.Exp, bias=nmax, accum_out=esum).then_inc(f_exp, 1)
            act.wait_ge(f_rest, f + 1)
            act.activation(E2, LGr[:, 0:TOK], ACT.Exp, bias=nmax).then_inc(f_exp2, 1)
            for b in range(2):
                act.wait_ge(f_pt, 2 * f + b + 1)
                act.activation(PTs[:, 4 * b:4 * b + 4, :].rearrange("p j m -> p (j m)"), psW[:, b, :], ACT.Copy)\
                    .then_inc(f_pts, 1)
            act.wait_ge(f_h, f + 1)
            act.activation(hid, T0[:, 0:32], ACT.Gelu).then_inc(f_gelu, 1)

        def ffn_dve(dve, f):
            if f == 0:
                dve.wait_ge(planes_zero, 16)
            dve.wait_ge(ffn_in, FFN_IN * (f + 1))
            dve.tensor_tensor(Gh.rearrange("p h (a e) -> p h a e", a=2),
                              graw.rearrange("p (h a e) -> p h a e", h=1, a=1).broadcast_to([128, 2, 2, EXP]),
                              const("half").rearrange("p (h a e) -> p h a e", h=2, e=1).broadcast_to(
                                  [128, 2, 2, EXP]), ALU.mult).then_inc(f_gw, 1)
            dve.wait_ge(f_gw, 2 * f + 1)
            dve.tensor_tensor(Gw.rearrange("p r h j -> p r (h j)"),
                              Gh.rearrange("p (o h) j -> p o (h j)", o=1).broadcast_to([128, R, 64]),
                              const("rowsel").rearrange("p (r o) -> p r o", o=1).broadcast_to([128, R, 64]),
                              ALU.mult).then_inc(f_gw, 1)
            dve.memset(LG[:, TOK:TOK + 8], LOW).then_inc(f_one, 1)
            dve.memset(pooled[32:33, :], 1.0).then_inc(f_one, 1)
            for b in range(2):
                dve.wait_ge(f_lg, 2 * f + b + 1)
                dve.tensor_scalar(LG[:, b * BANK:(b + 1) * BANK], psW[:, b, :], gb, None, ALU.add).then_inc(f_lgs, 1)
            dve.wait_ge(f_lgs, 2 * f + 2)
            dve.wait_ge(f_one, 2 * f + 2)
            dve.max(top8, LG[:, 0:TOK]).then_inc(f_top, 1)
            dve.wait_ge(f_top, f + 1)
            dve.tensor_tensor(spread.rearrange("p (q j) -> p q j", q=4),
                              top8.rearrange("p (q j) -> p q j", q=1).broadcast_to([128, 4, 8]),
                              const("quarter").rearrange("p (q j) -> p q j", j=1).broadcast_to([128, 4, 8]),
                              ALU.mult).then_inc(f_ex, 1)
            dve.wait_ge(f_cand, f + 1)
            dve.tensor_copy(cand, T0[0:32, 0:32]).then_inc(f_ct, 1)
            dve.wait_ge(f_ct, 3 * f + 1)
            dve.max(best, cand).then_inc(f_ct, 1)
            dve.wait_ge(f_ct, 3 * f + 2)
            dve.match_replace(cand_rest, best, cand, LOW).then_inc(f_ct, 1)
            dve.tensor_copy(pack[:, 32:33], best[:, 0:1]).then_inc(f_pack, 1)
            dve.wait_ge(f_ct, 3 * f + 3)
            dve.tensor_tensor(pack[:, 0:32], cand, cand_rest, ALU.not_equal).then_inc(f_pack, 1)
            dve.wait_ge(f_back, f + 1)
            dve.tensor_scalar(nmax, T1[:, 32:33], -1.0, None, ALU.mult).then_inc(f_max, 1)
            dve.tensor_tensor(picked.rearrange("p (q j) -> p q j", q=4),
                              T1[:, 0:32].rearrange("p (q j) -> p q j", q=4),
                              const("quarter").rearrange("p (q j) -> p q j", j=1).broadcast_to([128, 4, 8]),
                              ALU.mult).then_inc(f_msk, 1)
            dve.wait_ge(f_msk, 4 * f + 1)
            dve.tensor_reduce(keep, picked.rearrange("p (q j) -> p j q", q=4), AX_X, ALU.add).then_inc(f_msk, 1)
            dve.wait_ge(f_msk, 4 * f + 2)
            dve.tensor_scalar(drop, keep, -1.0, -LOW, ALU.add, ALU.mult).then_inc(f_msk, 1)
            dve.tensor_tensor(chosen, keep, top8, ALU.mult).then_inc(f_msk, 1)
            dve.wait_ge(f_msk, 4 * f + 4)
            dve.tensor_tensor(chosen, chosen, drop, ALU.add).then_inc(f_rden, 1)
            dve.wait_ge(f_rden, 2 * f + 1)
            dve.match_replace(LGr, chosen, LG, LOW).then_inc(f_rest, 1)
            dve.wait_ge(f_den, f + 1)
            dve.reciprocal(rden, T0[:, 0:1]).then_inc(f_rden, 1)
            dve.wait_ge(f_exp2, f + 1)
            for b in range(2):
                o = Pm[:, b * BANK:(b + 1) * BANK].rearrange("p (r y x) -> p r y x", r=R, y=2)
                s = [t[:, b * BANK:(b + 1) * BANK].rearrange("p (y r x) -> p r y x", y=2, r=R) for t in (Ee, E2)]
                dve.tensor_tensor(o, s[0], s[1], ALU.subtract).then_inc(f_dif, 1)
            dve.wait_ge(f_rden, 2 * f + 2)
            for b in range(2):
                dve.wait_ge(f_dif, 2 * f + b + 1)
                o = Pm[:, b * BANK:(b + 1) * BANK]
                dve.tensor_scalar(o, o, rden, None, ALU.mult).then_inc(f_p, 1)
            dve.wait_ge(f_pool, f + 1)
            dve.tensor_copy(pooled[0:32, :], T1[0:32, 0:32]).then_inc(f_pooled, 1)
            dve.wait_ge(f_o, f + 1)
            o = oexp.rearrange("p (n q e) -> p n q e", n=NI, q=4)
            for n in range(NI):
                ins = dve.tensor_tensor(
                    o[:, n], T1[0:32, 0:32].rearrange("p (e n) -> p n e", n=NI)[:, n:n + 1].broadcast_to([32, 4, EXP]),
                    W2b.rearrange("p (q e) -> p q e", q=1).broadcast_to([32, 4, EXP]), ALU.add)
            ins.then_inc(f_ob, 1)
            dve.wait_ge(f_ot, f + 1)
            for h in range(2):
                ins = dve.tensor_scalar(OB[:, h, :], T0[:, 0:32], const("parity")[:, h:h + 1], None, ALU.mult)
            ins.then_inc(f_obs, 1)
            for q in range(NQ):
                dve.wait_ge(f_y, NQ * f + q + 1)
                dve.tensor_tensor(bank(X, q), bank(X, q), bank(psA, q), ALU.add).then_inc(x_upd, 1)

        def dcn_pe(pe, l, pairs, chunks, shifts, word_reg):
            src = U if l == 0 else T2
            for k in range(R * NQ):
                q, r = divmod(k, R)
                if r == 0:
                    if l == 0:
                        pe.wait_ge(ln_out, 2 * NQ + q + 1)
                    else:
                        pe.wait_ge(d_bn, q + 1)
                if k == 0:
                    pe.wait_ge(bd_ready, 5)
                if k >= 4:
                    who, n = OM_OUT[k - 4]
                    pe.wait_ge(d_oma if who == "act" else d_omv, (OM_ACT if who == "act" else 4) * l + n)
                pe.matmul([psW[:, 0], psW[:, 1], T0, T1][k % 4][0:108, :], Wom4[:, r, :], bank(src, q),
                          start=True, stop=True).then_inc(d_om, 1)
            for q in range(NQ):
                pe.matmul(bank(psA, q), Wv_bd[:, :], bank(src, q), start=True, stop=True).then_inc(d_val, 1)
            pe.wait_ge(z_bank, l + 2)
            pe.wait_ge(d_vals, NQ * (l + 1))
            pe.wait_ge(d_oma, OM_ACT * (l + 1))
            pe.wait_ge(d_omv, 4 * (l + 1))
            pe.wait_ge(d_kext, 2 * (l + 1))
            for kind in range(2):
                for g in range(G):
                    at = g * 27 + kind * 9
                    mm = pe.matmul(T0[0:9, kind * 8 + g:kind * 8 + g + 5:4], ident[0:108, at:at + 9], ext[0:108, :],
                                   start=True, stop=True, skip_group_check=True)
            mm.then_inc(d_tr, 1)
            pe.wait_ge(d_reach, 2 * (l + 1))
            for h in range(2):
                for g in range(G):
                    mm = pe.matmul(T1[0:NYP, h * NACT:(h + 1) * NACT], cmp_y[0][:, g, h * NYP:(h + 1) * NYP],
                                   cmp_x[0][:, g, :], start=g == 0, stop=g == G - 1, skip_group_check=True)
            mm.then_inc(d_act, 1)
            pe.matmul(psW[:, 0, 0:256], ident, zero_bank[:, 0:256], start=True, stop=True, skip_group_check=True)\
                .then_inc(w_sum, 1)
            pe.matmul(psW[:, 1, 0:256], ident, zero_bank[:, 0:256], start=True, stop=True, skip_group_check=True)\
                .then_inc(w_sum, 1)
            for q in range(NQ):
                pe.matmul(bank(psA, q), ident, zero_bank, start=True, stop=True, skip_group_check=True)\
                    .then_inc(acc_zero, 1)
            pe.wait_ge(acc_zero, NQ * (l + 1))
            pe.sem_inc(acc_sum, 1)
            if l > 0:
                pe.reg_add(shifts, shifts, LEAD)
            pe.wait_ge(d_rng, l + 1)
            pe.wait_ge(words_in, 16 * (l + 1))

            def add_values(n, i):
                pe.wait_ge(m_ready, n + (LEAD + i + 1))
                for q in range(NQ):
                    mm = pe.matmul(bank(psA, q), ident, bank(Mt[:, i % 2], q), start=False, stop=True,
                                   skip_group_check=True)
                mm.then_inc(acc_sum, 1)

            def sums(cx, iy, nch, done):
                w = load_word(pe, word_reg, cx, iy)
                for h in range(2):
                    lo, hi, full, off = row_fields(pe, w, h)

                    def run(kind):
                        left = kind[0] - kind[1] - sum(kind[2])
                        with pe.Fori(lo, hi):
                            n = pe.snap(shifts)
                            for i in range(2):
                                pe.wait_ge(p_ready, n + (LEAD + i + 1))
                                for k in range(left):
                                    mm = pe.matmul(psW[:, i, 0:256], ident, Pt[:, i, k * 256:(k + 1) * 256],
                                                   start=k == 0, stop=k == left - 1, skip_group_check=True)
                                mm.then_inc(w_sum, 1)
                                add_values(n, i - 1)
                            pe.reg_add(shifts, shifts, 2)

                    by_kind(pe, full, run)

            walk(pe, pairs, chunks, sums)
            add_values(pe.snap(shifts), -1)
            for q in range(NQ):
                if q == 0:
                    pe.wait_ge(d_smp, NQ * (l + 1))
                if q % 2 == 0:
                    pe.wait_ge(d_smld[q // 2], 16 * G * (l + 1))
                pe.matmul(bank(psA, q), Wo_bd[:, :], bank(VAL, q), start=True, stop=True).then_inc(d_wo, 1)
            pe.wait_ge(d_agg, l + 1)
            pe.matmul(T0[:, 0:1], const("row_mean"), small[:, 8:9], start=True, stop=True).then_inc(d_mean, 1)
            pe.wait_ge(d_dev, 3 * l + 3)
            pe.matmul(T1[:, 0:1], const("row_mean"), small[:, 10:11], start=True, stop=True).then_inc(d_varm, 1)
            if l == 1:
                for q in range(NQ):
                    pe.wait_ge(d_zs, q + 1)
                    pe.matmul(bank(psA, q), Wc_bd[:, :], bank(Zt, q), start=True, stop=True).then_inc(d_wc, 1)

        def dcn_act(act, l, pairs, chunks, abses, start_pair, word_reg):
            for k in range(R * NQ):
                if OM_OUT[k][0] == "act":
                    act.wait_ge(d_om, 16 * l + k + 1)
                    if k == 0:
                        act.wait_ge(bd_ready, 5)
                    act.activation(om_rows(k), om_bank(k), ACT.Identity, bias=vecs[0:108, 3:4]).then_inc(d_oma, 1)
            for q in range(NQ):
                act.wait_ge(d_val, NQ * l + q + 1)
                if l == 1 and q == 0:
                    act.wait_ge(d_wo, NQ)
                act.activation(bank(VAL, q), bank(psA, q), ACT.Identity, bias=vecs[:, 0:1]).then_inc(d_vals, 1)
            act.wait_ge(d_rng, l + 1)

            def hat(dst, src, shift, done):
                act.activation(dst, src, ACT.Abs, bias=shift).then_inc(hat_abs, 1)
                act.wait_ge(hat_abs, act.snap(abses) + 1)
                act.reg_add(abses, abses, 1)
                act.activation(dst, dst, ACT.Relu, bias=1.0, scale=-1.0).then_inc(done, 1)

            def row_hat(iy, h, done):
                act.wait_ge(ay_free, done * 2 + (h + 1))
                hat(ay[:, h, :], dy, const("ytab")[:, bass.ds(iy * 2 + h, 1)], ay_ready)

            def first_hats(cx, iy, nch, done):
                act.wait_ge(d_dxy, 128 * (l + 1))
                act.wait_ge(d_short, 16)
                row_hat(iy, 0, done)
                act.wait_ge(words_in, 16 * (l + 1))
                act.reg_mov(start_pair, load_word(act, word_reg, cx, iy) & 7)
                act.wait_ge(hx_free, nch + 1)
                act.wait_ge(d_vst, 128 * (l + 1))
                for jp in range(XP):
                    pair = hold(act, (act.snap(start_pair) + jp) % XP, 0, XP - 1)
                    for i in range(1 if jp == 0 else 0, 2):
                        c = pair * 2 + i
                        hat(hxs[:, bass.ds(c * TAPS, TAPS)], dx, const("xtab")[:, bass.ds(cx * XC + c, 1)], hx_ready)
                    if jp == 2:
                        row_hat(iy, 1, done)

            def row_hats(cx, iy, nch, done):
                for h in range(2):
                    row_hat(iy, h, done)

            walk(act, pairs, chunks, row_hats, first=first_hats)
            act.wait_ge(d_acc, l + 1)
            for q in range(1, NQ, 2):
                act.activation(bank(SMP, q), bank(psA, q), ACT.Copy).then_inc(d_smp, 1)
            act.wait_ge(d_varm, l + 1)
            act.wait_ge(d_dev, 3 * l + 3)
            act.activation(small[:, 11:12], T1[:, 0:1], ACT.Sqrt, bias=const("eps5")).then_inc(d_std, 1)
            act.wait_ge(d_sc, 4 * l + 4)
            for q in range(NQ):
                if l == 0:
                    act.activation(bank(T2, q), bank(psA, q), ACT.Relu, bias=small[:, 14:15],
                                   scale=small[:, 13:14]).then_inc(d_bn, 1)
                else:
                    act.activation(bank(Zt, q), bank(psA, q), ACT.Identity, bias=small[:, 14:15],
                                   scale=small[:, 13:14]).then_inc(d_bn, 1)

        OWN_STEPS = 37

        def dcn_dve(dve, l, pairs, chunks, shifts, mults, column, turn, word_reg):
            if l == 0:
                dve.wait_ge(small_in, 16 * (4 * R + G + 3))
                rs, cs = const("rowsel"), const("colsel")
                dve.tensor_tensor(Wv_bd[:, :].rearrange("p (g r c) -> p g r c", g=G, r=R),
                                  raw1[:, 0, :].rearrange("p (g r c) -> p g r c", g=G, r=1).broadcast_to(
                                      [128, G, R, CG]),
                                  rs.rearrange("p (g r c) -> p g r c", g=1, c=1).broadcast_to([128, G, R, CG]),
                                  ALU.mult).then_inc(bd_ready, 1)
                for w, i, s in ((Wo_bd, 1, cs), (Wc_bd, 2, rs)):
                    dve.tensor_tensor(w[:, :].rearrange("p (r c) -> p r c", r=R),
                                      raw1[:, i, :].rearrange("p (r c) -> p r c", r=1).broadcast_to([128, R, C]),
                                      s.rearrange("p (r c) -> p r c", c=1).broadcast_to([128, R, C]),
                                      ALU.mult).then_inc(bd_ready, 1)
                dve.tensor_tensor(Wom4[:, :, :], Wom_r.rearrange("p (r j) -> p r j", r=1).broadcast_to([128, R, 108]),
                                  rs.rearrange("p (r j) -> p r j", j=1).broadcast_to([128, R, 108]),
                                  ALU.mult).then_inc(bd_ready, 1)
                dve.tensor_tensor(vecs[0:108, 3:4], vecs[0:108, 3:4], const("tapoff", 108), ALU.add)\
                    .then_inc(bd_ready, 1)
                dve.wait_ge(bd_ready, 5)
            if l == 0:
                dve.memset(ext, 0.0).then_inc(z_bank, 1)
            dve.memset(zero_bank, 0.0).then_inc(z_bank, 1)
            dve.memset(Vt[:, 1], 0.0).then_inc(v_zero, 1)
            for k in range(R * NQ):
                if OM_OUT[k][0] == "dve":
                    dve.wait_ge(d_om, 16 * l + k + 1)
                    dve.tensor_scalar(om_rows(k), om_bank(k), vecs[0:108, 3:4], None, ALU.add).then_inc(d_omv, 1)
            own = [0]

            def step(ins):
                ins.then_inc(d_cmp, 1)
                own[0] += 1

            def settle():
                dve.wait_ge(d_cmp, OWN_STEPS * l + own[0])

            for n in range(NI):
                dve.wait_ge(d_oma, OM_ACT * l + (4 if n == 0 else OM_ACT))
                if n == 0:
                    dve.wait_ge(d_omv, 4 * (l + 1))
                for i, op in enumerate((ALU.min, ALU.max)):
                    step(dve.tensor_reduce(ext_half[0:108, 2 * i + n:2 * i + n + 1],
                                           OMs[:, n].rearrange("p y r x -> p (y r x)"), AX_X, op))
            settle()
            dve.wait_ge(z_bank, l + 2)
            step(dve.tensor_tensor(ext[0:108, 0:1], ext_half[0:108, 0:1], ext_half[0:108, 1:2], ALU.min))
            settle()
            dve.tensor_scalar(ext[0:108, 0:1], ext[0:108, 0:1], -1.0, None, ALU.mult).then_inc(d_kext, 1)
            dve.tensor_tensor(ext[0:108, 1:2], ext_half[0:108, 2:3], ext_half[0:108, 3:4], ALU.max)\
                .then_inc(d_kext, 1)
            dve.wait_ge(d_kext, 2 * (l + 1))
            dve.tensor_scalar(small[:, 0:2], ext, const("notx"), None, ALU.add).then_inc(d_ext, 1)
            dve.tensor_scalar(small[:, 2:4], ext, const("noty"), None, ALU.add).then_inc(d_ext, 1)
            dve.wait_ge(d_tr, l + 1)
            step(dve.tensor_copy(ext_g, T0[0:9, 0:16].rearrange("p (i g) -> p i g", i=4)))
            settle()
            ny, nx = 2 * NYP, XP * NXC
            for out_, names, kind, w in ((cmp_y, ("yabove", "ybelow"), 2, ny), (cmp_x, ("xabove", "xbelow"), 0, nx)):
                for i in range(2):
                    step(dve.tensor_tensor(out_[i][:, :, 0:w],
                                           const(names[i], 9).rearrange("p (g s) -> p g s", g=1).broadcast_to([9, G, w]),
                                           ext_g[:, kind + i, :].rearrange("p (g s) -> p g s", s=1).broadcast_to(
                                               [9, G, w]), ALU.is_lt))
            step(dve.tensor_copy(cmp_x[0][:, :, nx:nx + 3],
                                 const("taprow", 9).rearrange("p (g s) -> p g s", g=1).broadcast_to([9, G, 3])))
            settle()
            dve.tensor_tensor(cmp_y[0], cmp_y[0], cmp_y[1], ALU.mult).then_inc(d_reach, 1)
            dve.tensor_tensor(cmp_x[0][:, :, 0:nx], cmp_x[0][:, :, 0:nx], cmp_x[1][:, :, 0:nx], ALU.mult)\
                .then_inc(d_reach, 1)
            dve.wait_ge(d_all, l + 1)
            tabs = ((const("xlow", 1), ALU.is_ge), (const("xhigh", 1), ALU.is_lt),
                    (const("yabove", 1)[:, NYP:2 * NYP], ALU.is_ge), (const("ybelow", 1)[:, 0:NYP], ALU.is_lt))
            at = [0, NXC, 2 * NXC, 2 * NXC + NYP]
            rt = area(36700, 40)[0:1, :]
            for i, (tab, op) in enumerate(tabs):
                step(dve.tensor_scalar(rng_cmp[:, at[i]:at[i] + tab.shape[1]], tab, small[0:1, 4 + i:5 + i], None, op))
            settle()
            for i, (tab, op) in enumerate(tabs):
                step(dve.tensor_reduce(rt[:, i:i + 1], rng_cmp[:, at[i]:at[i] + tab.shape[1]], AX_X,
                                       ALU.add))
            settle()
            for i in range(4):
                n = NXC if i < 2 else NYP
                lo, hi = (0.0, n - 1.0) if i % 2 == 0 else (1.0, float(n))
                step(dve.tensor_scalar(rt[:, 4 + i:5 + i], rt[:, i:i + 1], lo, hi, ALU.max, ALU.min))
            settle()
            dve.tensor_copy(ranges[:, :], rt[:, 4:8]).then_inc(d_rng, 1)
            dve.wait_ge(d_act, l + 1)
            step(dve.tensor_scalar(reach, T1[0:NYP, 0:2 * NACT].rearrange("p (h s) -> p h s", h=2), 0.0, None,
                                   ALU.is_gt))
            settle()
            for name, dst in (("fromend", first), ("fromstart", last)):
                step(dve.tensor_tensor(scaled, reach[:, :, 0:nx],
                                       const(name, NYP).rearrange("p (h s) -> p h s", h=1).broadcast_to([NYP, 2, nx]),
                                       ALU.mult))
                settle()
                step(dve.tensor_reduce(dst, scaled.rearrange("p h (c j) -> p h c j", j=XP), AX_X, ALU.max))
                settle()
            b0, b2 = reach[:, :, nx:nx + 1], reach[:, :, nx + 2:nx + 3]
            k0, k1 = kinds[:, 0, :].rearrange("p (h o) -> p h o", o=1), kinds[:, 1, :].rearrange("p (h o) -> p h o", o=1)
            step(dve.tensor_scalar(last, last, 1.0, None, ALU.max))
            step(dve.tensor_scalar(first, first, -1.0, float(XP), ALU.mult, ALU.add))
            step(dve.tensor_tensor(k0, b0, b2, ALU.mult))
            step(dve.tensor_scalar(k1, b0, -128.0, 128.0, ALU.mult, ALU.add))
            settle()
            step(dve.scalar_tensor_tensor(out=first, in0=last, scalar=-1.0, in1=first, op0=ALU.add, op1=ALU.min))
            step(dve.scalar_tensor_tensor(out=k1, in0=k0, scalar=64.0, in1=k1, op0=ALU.mult, op1=ALU.add))
            settle()
            step(dve.scalar_tensor_tensor(out=word, in0=last, scalar=8.0, in1=first, op0=ALU.mult, op1=ALU.add))
            settle()
            step(dve.tensor_tensor(word, word, k1.broadcast_to([NYP, 2, NXC]), ALU.add))
            settle()
            step(dve.scalar_tensor_tensor(out=packed, in0=word[:, 1, :], scalar=256.0, in1=word[:, 0, :],
                                          op0=ALU.mult, op1=ALU.add))
            settle()
            dve.tensor_copy(packed_i, packed).then_inc(d_words, 1)
            assert own[0] == OWN_STEPS, own[0]
            if l == 0:
                dve.sem_inc(v_free[0], 1)
                dve.sem_inc(acc_sum, 1)
                dve.sem_inc(hx_ready, 1)
                dve.sem_inc(ay_masked, 1)
                dve.sem_inc(hx_free, 1)
                dve.sem_inc(ay_free, 1)
            dve.sem_inc(p_part, LEAD)
            dve.sem_inc(m_ready, 1)
            if l > 0:
                dve.reg_add(shifts, shifts, LEAD)
            dve.reg_mov(column, 0)
            dve.wait_ge(v_zero, l + 1)
            dve.wait_ge(d_rng, l + 1)
            dve.wait_ge(d_words, l + 1)

            def product(h, c, n, i, hats, off, kind):
                taps, fold, _ = kind
                w = taps * R * HW
                dve.wait_ge(hx_ready, hats + (i + 2))
                dve.wait_ge(w_sum, n + (LEAD + i - 1))
                made = dve.tensor_tensor(Pt[:, i, 0:w], ay[:, h, bass.ds(off, w)] if taps < K else ay[:, h, :],
                                         hxs[:, bass.ds(c * TAPS + off if taps < K else c * TAPS, w)], ALU.mult)
                if fold:
                    made.then_inc(p_mult, 1)
                    dve.reg_add(mults, mults, 1)
                    dve.wait_ge(p_mult, dve.snap(mults))
                    dve.tensor_tensor(*fold_taps(i, taps, fold)).then_inc(p_part, 1)
                else:
                    made.then_inc(p_part, 1)

            def weigh(h, c, n, i):
                dve.wait_ge(w_sum, n + (LEAD + i + 1))
                dve.wait_ge(acc_sum, n + (LEAD + i))
                w = psW[:, i % 2, 0:256].rearrange("p (r o x) -> p r o x", r=R, o=1)
                dve.tensor_tensor(Mt[:, i % 2].rearrange("p (r c x) -> p r c x", r=R, c=CG),
                                  Vt[:, h, :, bass.ds(c, HW)].rearrange("p (r c) x -> p r c x", r=R),
                                  w.broadcast_to([128, R, CG, HW]), ALU.mult).then_inc(m_ready, 1)

            def find_start(cx, iy, nch):
                dve.wait_ge(words_in, 16 * (l + 1))
                dve.wait_ge(d_dxy, 128 * (l + 1))
                pair = load_word(dve, word_reg, cx, iy) & 7
                dve.reg_mov(turn, (pair * -1 + XP) & 7)
                c = hold(dve, pair * 2, 0, XC - 2)
                h0 = hxs[:, bass.ds(c * TAPS, TAPS)]
                shift = const("xtab")[:, bass.ds(cx * XC + c, 1)]
                n = hold(dve, nch * 3, 0, 1 << 20)
                dve.wait_ge(d_vst, 128 * (l + 1))
                dve.wait_ge(hx_ready, nch * XC + 1)
                dve.tensor_scalar(h0, dx, shift, None, ALU.add).then_inc(hat_dve, 1)
                dve.wait_ge(hat_dve, n + 1)
                dve.scalar_tensor_tensor(out=h0, in0=h0, scalar=-1.0, in1=h0, op0=ALU.mult, op1=ALU.min)\
                    .then_inc(hat_dve, 1)
                dve.wait_ge(hat_dve, n + 2)
                dve.tensor_scalar(h0, h0, 1.0, 0.0, ALU.add, ALU.max).then_inc(hat_dve, 1)
                dve.wait_ge(hat_dve, n + 3)
                dve.sem_inc(hx_ready, 1)

            def hats_before(nch, jp):
                return hold(dve, nch * XC + ((dve.snap(turn) + jp) % XP) * 2, 0, 1 << 20)

            def weights(cx, iy, nch, done):
                word_now = load_word(dve, word_reg, cx, iy)
                for h in range(2):
                    lo, hi, full, off = row_fields(dve, word_now, h)

                    def run(kind):
                        n = dve.snap(shifts)
                        c = hold(dve, lo * 2, 0, XC - 2)
                        hats = hats_before(nch, lo)
                        dve.wait_ge(ay_masked, done * 6 + (3 * h + 4))
                        product(h, c, n, 0, hats, off, kind)
                        dve.wait_ge(p_part, n + LEAD)
                        dve.sem_inc(ay_free, 1)
                        weigh(1 - h, dve.snap(column, min_val=0, max_val=XC - 1), n, -1)
                        product(h, c + 1, n, 1, hats, off, kind)
                        dve.wait_ge(m_ready, n + LEAD)
                        dve.sem_inc(v_free[1 - h], 1)
                        dve.wait_ge(v_loaded[h], done * 128 + 128)
                        weigh(h, c, n, 0)
                        dve.reg_add(shifts, shifts, 2)
                        with dve.If(lo + 1 < hi):
                            with dve.Fori(lo + 1, hi) as jp:
                                n = dve.snap(shifts)
                                c = hold(dve, jp * 2, 2, XC - 2)
                                hats = hats_before(nch, jp)
                                product(h, c, n, 0, hats, off, kind)
                                weigh(h, hold(dve, jp * 2 - 1, 1, XC - 3), n, -1)
                                product(h, c + 1, n, 1, hats, off, kind)
                                weigh(h, c, n, 0)
                                dve.reg_add(shifts, shifts, 2)
                            dve.nop()

                    by_kind(dve, full, run)
                    dve.reg_mov(column, hi * 2 - 1)

            def chunk_done():
                dve.wait_ge(p_part, dve.snap(shifts) + LEAD)
                dve.sem_inc(hx_free, 1)

            walk(dve, pairs, chunks, weights, start=find_start, chunk_end=chunk_done)
            n = dve.snap(shifts)
            weigh(1, dve.snap(column, min_val=0, max_val=XC - 1), n, -1)
            dve.wait_ge(acc_sum, n + (LEAD + 1))
            dve.wait_ge(p_part, n + LEAD)
            dve.sem_inc(d_acc, 1)
            for q in range(0, NQ, 2):
                dve.tensor_copy(bank(SMP, q), bank(psA, q)).then_inc(d_smp, 1)
            for q in range(NQ):
                dve.wait_ge(d_wo, NQ * l + q + 1)
                dve.bn_stats(stats[:, q, :], bank(psA, q)).then_inc(d_st, 1)
            dve.wait_ge(d_st, NQ * (l + 1))
            dve.bn_aggr(small[:, 8:10], stats[:, :, :]).then_inc(d_agg, 1)
            dve.wait_ge(d_mean, l + 1)
            dve.tensor_tensor(small[:, 12:13], small[:, 8:9], T0[:, 0:1], ALU.subtract).then_inc(d_dev, 1)
            dve.wait_ge(d_dev, 3 * l + 1)
            dve.tensor_tensor(small[:, 12:13], small[:, 12:13], small[:, 12:13], ALU.mult).then_inc(d_dev, 1)
            dve.wait_ge(d_dev, 3 * l + 2)
            dve.wait_ge(d_agg, l + 1)
            dve.tensor_tensor(small[:, 10:11], small[:, 12:13], small[:, 9:10], ALU.add).then_inc(d_dev, 1)
            dve.wait_ge(d_std, l + 1)
            dve.reciprocal(small[:, 13:14], small[:, 11:12]).then_inc(d_sc, 1)
            dve.wait_ge(d_sc, 4 * l + 1)
            dve.tensor_tensor(small[:, 13:14], small[:, 13:14], vecs[:, 1:2], ALU.mult).then_inc(d_sc, 1)
            dve.wait_ge(d_sc, 4 * l + 2)
            dve.tensor_tensor(small[:, 15:16], T0[:, 0:1], small[:, 13:14], ALU.mult).then_inc(d_sc, 1)
            dve.wait_ge(d_sc, 4 * l + 3)
            dve.tensor_tensor(small[:, 14:15], vecs[:, 2:3], small[:, 15:16], ALU.subtract).then_inc(d_sc, 1)
            if l == 1:
                dve.wait_ge(d_shld, 16)
                for q in range(NQ):
                    dve.wait_ge(d_bn, NQ + q + 1)
                    dve.tensor_tensor(bank(Zt, q), bank(Zt, q), bank(SHT, q), ALU.add).then_inc(d_zs, 1)
                for q in range(NQ):
                    dve.wait_ge(d_wc, q + 1)
                    dve.tensor_tensor(bank(X, q), bank(X, q), bank(psA, q), ALU.add).then_inc(x_upd, 1)

        LN_FOR = [(0, x_loaded, "eps6"), (1, x_updated(0), "eps5"), (2, x_updated(1), "eps6"),
                  (3, x_updated(2), "eps5")]

        @block.tensor
        def _(pe):
            pe.wait_ge(ln_cst_in, 16)
            pairs, chunks, shifts, word_reg = counters(pe, ("pairs_run", "chunks_run", "shifts_run", "word"))
            ln_pe(pe, 0, X, x_loaded)
            unet_pe(pe)
            pe.wait_ge(cst_in, 16)
            ln_pe(pe, 1, X, x_updated(0))
            ffn_pe(pe, 0)
            ln_pe(pe, 2, X, x_updated(1))
            for l in range(2):
                dcn_pe(pe, l, pairs, chunks, shifts, word_reg)
            ln_pe(pe, 3, X, x_updated(2))
            ffn_pe(pe, 1)

        @block.scalar
        def _(act):
            act.wait_ge(ln_cst_in, 16)
            pairs, chunks, abses, start_pair, word_reg = counters(
                act, ("pairs_run", "chunks_run", "abses_run", "start_pair", "word"))
            banded_act(act)
            ln_act(act, 0, "eps6")
            unet_act(act)
            act.wait_ge(cst_in, 16)
            ln_act(act, 1, "eps5")
            ffn_act(act, 0)
            ln_act(act, 2, "eps6")
            for l in range(2):
                dcn_act(act, l, pairs, chunks, abses, start_pair, word_reg)
            ln_act(act, 3, "eps5")
            ffn_act(act, 1)

        @block.vector
        def _(dve):
            dve.wait_ge(ln_cst_in, 16)
            pairs, chunks, shifts, mults, column, turn, word_reg = counters(
                dve, ("pairs_run", "chunks_run", "shifts_run", "mults_run", "last_column", "turn", "word"))
            for t in A + B + D:
                ny, w = t.shape[2], t.shape[3]
                dve.memset(t[:, :, 0:ny:ny - 1, :], 0.0).then_inc(borders, 1)
                dve.memset(t[:, :, 1:ny - 1, 0:w:w - 1], 0.0).then_inc(borders, 1)
            banded_dve(dve)
            ln_dve(dve, 0, X, x_loaded,
                   lambda q: inner(A[0], q // 2, 1 + q % 2 * 8, 8, 1, 1)[:, 0])
            unet_dve(dve)
            dve.wait_ge(cst_in, 16)
            ln_dve(dve, 1, X, x_updated(0), lambda q: bank(U, q))
            ffn_dve(dve, 0)
            ln_dve(dve, 2, X, x_updated(1), lambda q: bank(U, q))
            for l in range(2):
                dcn_dve(dve, l, pairs, chunks, shifts, mults, column, turn, word_reg)
            ln_dve(dve, 3, X, x_updated(2), lambda q: bank(U, q))
            ffn_dve(dve, 1)


def prepare(inputs):
    def a(name):
        return np.asarray(inputs[name])

    w3 = np.stack([a("L0_conv_" + n) for n in S1 + S2])
    w3 = w3.transpose(2, 0, 4, 3, 1)[:, :, :, ::-1, :].reshape(C, RAW3)
    ds = np.stack([a("L0_conv_" + n)[:, :, 0, 0] for n in DS]).transpose(2, 0, 1).reshape(C, 64)
    dec = np.stack([a("L0_conv_" + n) for n in DEC]).transpose(1, 0, 4, 3, 2).reshape(C, 256)
    wom = a("L1_conv_Wom").reshape(C, G, 27)
    bom = a("L1_conv_bom").reshape(1, G, 27)

    def planes(t):
        off = t[:, :, 0:18].reshape(-1, G, K, 2).transpose(0, 1, 3, 2).reshape(-1, G, 18)
        return np.concatenate([off, t[:, :, 18:27]], axis=2).reshape(-1, 108)

    arrays = {
        "x": a("x"),
        "convw": np.concatenate([w3, ds, dec], axis=1),
        "gate_w": np.stack([a(f"L{f}_ffn_gate_w").T for f in range(2)]),
        "gate_b": np.stack([a(f"L{f}_ffn_gate_b") for f in range(2)]),
        "w1": np.stack([a(f"L{f}_ffn_weight1") for f in range(2)]),
        "w2": np.stack([a(f"L{f}_ffn_weight2") for f in range(2)]),
        "w2b": np.stack([a(f"L{f}_ffn_weight2")[:, HID, :].T for f in range(2)]),
        "wv": a("L1_conv_Wv"),
        "bv": a("L1_conv_bv"),
        "wom": planes(wom),
        "bom": planes(bom)[0],
        "wo": a("L1_conv_Wo"),
        "gamma": a("L1_conv_gamma"),
        "beta": a("L1_conv_beta"),
        "wct": a("L1_conv_Wc").T,
        "consts": constants(),
    }
    return {k: np.ascontiguousarray(v) for k, v in arrays.items()}


def kernel(**inputs):
    import concourse.bacc as _bacc
    from concourse.bass_utils import run_bass_kernel_spmd as _run

    nc = _bacc.Bacc("TRN2", target_bir_lowering=False, num_devices=1)
    arrays, args = {}, []
    for name, a in prepare(inputs).items():
        arrays[f"in_{name}"] = a
        args.append(nc.dram_tensor(f"in_{name}", a.shape, mybir.dt.from_np(a.dtype), kind="ExternalInput").ap())
    out = nc.dram_tensor("out_x", (NI, C, HW, HW), F32, kind="ExternalOutput").ap()
    metaformer_kernel(nc, *args, out)
    return _run(nc, [arrays], core_ids=[0]).results[0]["out_x"]
```
